# Optimizing a Trainium2 kernel written in Bass

```python
import numpy as np
import jax
import jax.numpy as jnp

def _softmax(x, axis=-1):
    return jax.nn.softmax(x, axis=axis)

def _gelu(x):
    return jax.nn.gelu(x, approximate=True)

def _silu(x):
    return jax.nn.silu(x)

def _sigmoid(x):
    return jax.nn.sigmoid(x)

def _layernorm(x, axis=-1, eps=1e-05):
    m = jnp.mean(x, axis=axis, keepdims=True)
    v = jnp.var(x, axis=axis, keepdims=True)
    return (x - m) / jnp.sqrt(v + eps)

def _scatter_add(tgt, idx, src, axis=0):
    return tgt.at[idx].add(src)

def _segment_sum(src, seg, n):
    return jax.ops.segment_sum(src, seg, n)
kernel_name = 'mk_gnn_preln_d1_gnn_r8_563013'

def setup_inputs(seed: int=0):
    np.random.seed(seed)
    _w = jnp.asarray

    def _rec_inputs():
        import jax
        import jax.numpy as jnp
        _gk = jax.random.key(seed)
        x = -0.000202 + 1 * jax.random.normal(jax.random.fold_in(_gk, 1), (12500, 128), jnp.float32)
        _s = jax.random.randint(jax.random.fold_in(_gk, 2), (200000,), 0, 12500, jnp.int32)
        _d = jax.random.randint(jax.random.fold_in(_gk, 3), (200000,), 0, 12500, jnp.int32)
        _loop = jnp.arange(12500, dtype=jnp.int32)
        src = jnp.concatenate([_s, _d, _loop])
        dst = jnp.concatenate([_d, _s, _loop])
        _o = jnp.argsort(dst, stable=True)
        src = src[_o]
        dst = dst[_o]
        edge_attr_64 = 0.000189758 + 1.00013 * jax.random.normal(jax.random.fold_in(_gk, 11), (412500, 64), jnp.float32)
        return (x, src, dst, edge_attr_64)
    x, src, dst, edge_attr_64 = _rec_inputs()

    def _L0_gnn_setup():
        import jax, jax.numpy as jnp
        import numpy as np
        N_NODES = 6250
        N_EDGES = 100000
        F_NODE = 128
        F_EDGE = 64
        MSG = 32
        key = jax.random.key(seed)
        k1, k2, k3, k4, k5, k6, k7 = jax.random.split(key, 7)
        node_features = jax.random.normal(k1, (N_NODES, F_NODE), dtype=jnp.float32)
        edge_node_indices = jax.random.randint(k2, (2, N_EDGES), 0, N_NODES, dtype=jnp.int64)
        edge_features = jax.random.normal(k3, (N_EDGES, F_EDGE), dtype=jnp.float32)
        edge_in = 2 * F_NODE + F_EDGE
        node_in = F_NODE + MSG
        W_edge = jax.random.uniform(k4, (edge_in, MSG), dtype=jnp.float32, minval=-1.0, maxval=1.0) / np.sqrt(edge_in)
        b_edge = jax.random.uniform(k5, (MSG,), dtype=jnp.float32, minval=-1.0, maxval=1.0) / np.sqrt(edge_in)
        W_node = jax.random.uniform(k6, (node_in, F_NODE), dtype=jnp.float32, minval=-1.0, maxval=1.0) / np.sqrt(node_in)
        b_node = jax.random.uniform(k7, (F_NODE,), dtype=jnp.float32, minval=-1.0, maxval=1.0) / np.sqrt(node_in)
        return {'node_features': node_features, 'edge_node_indices': edge_node_indices, 'edge_features': edge_features, 'W_edge': W_edge, 'b_edge': b_edge, 'W_node': W_node, 'b_node': b_node}
    _L0_gnn_all = _L0_gnn_setup()
    _L0_gnn_in = {k: v for k, v in _L0_gnn_all.items() if k in ('W_edge', 'b_edge', 'W_node', 'b_node')}
    del _L0_gnn_all
    return {'x': x, 'src': src, 'dst': dst, 'edge_attr_64': edge_attr_64, 'L0_gnn_W_edge': _L0_gnn_in['W_edge'], 'L0_gnn_b_edge': _L0_gnn_in['b_edge'], 'L0_gnn_W_node': _L0_gnn_in['W_node'], 'L0_gnn_b_node': _L0_gnn_in['b_node']}

def reference(x, src, dst, edge_attr_64, L0_gnn_W_edge, L0_gnn_b_edge, L0_gnn_W_node, L0_gnn_b_node):
    import jax
    import jax.numpy as jnp

    def _L0_gnn_ref(node_features, edge_node_indices, edge_features, W_edge, b_edge, W_node, b_node):
        import jax, jax.numpy as jnp
        import numpy as np
        N_NODES = 6250
        N_EDGES = 100000
        F_NODE = 128
        F_EDGE = 64
        MSG = 32
        node0 = edge_node_indices[0]
        node1 = edge_node_indices[1]
        message_input = jnp.concatenate([node_features[node0], node_features[node1], edge_features], axis=1)
        messages = jax.nn.relu(message_input @ W_edge + b_edge)
        msg_sums = jax.ops.segment_sum(messages, node0, num_segments=node_features.shape[0])
        node_input = jnp.concatenate([node_features, msg_sums], axis=1)
        return jax.nn.relu(node_input @ W_node + b_node)
    edge_index = jnp.stack([src, dst])
    h = jnp.maximum(_layernorm(x, axis=-1), 0.0)
    x = x + _L0_gnn_ref(h, edge_index, edge_attr_64, L0_gnn_W_edge, L0_gnn_b_edge, L0_gnn_W_node, L0_gnn_b_node)
    return x

_drawn_inputs = setup_inputs


def setup_inputs(seed=0):
    import zlib

    import numpy as np

    out = dict(_drawn_inputs(seed))
    spreads = {}
    factors = {'L0_gnn_b_node': 2.749}
    for name, (base, spread) in spreads.items():
        noise = np.random.default_rng([zlib.crc32(name.encode()), seed]).standard_normal(out[name].shape)
        drawn = base * np.exp(spread * noise) if base else spread * noise
        out[name] = jnp.asarray(drawn.astype(out[name].dtype))
    for name, factor in factors.items():
        out[name] = (out[name] * factor).astype(out[name].dtype)
    return out
```

```python
import concourse.bass as bass
from concourse import mybir
from contextlib import ExitStack


def gnn_layer(nc, x, src, dst, ef, w_edge, b_edge, w_node, b_node, y):
    f32, bf16, i32 = mybir.dt.float32, mybir.dt.bfloat16, mybir.dt.int32
    ALU = mybir.AluOpType
    ACT = mybir.ActivationFunctionType
    AX = mybir.AxisListType.X
    ds = bass.ds

    P = 128
    N, F = x.shape
    E, FE = ef.shape
    M = w_edge.shape[1]
    J = 4
    T = P * J
    NS = -(-E // T)
    LAST0 = E - T
    SEEN = (NS * T - E) // J
    assert (NS * T - E) % J == 0 and NS % 2 == 0
    SB = -(-NS // P)
    NB = -(-N // P)
    NTAIL = N - (NB - 1) * P
    NS2 = -(-(E // T + NB + 1) // 8) * 8
    assert NS2 * T >= E + NB * (T - 1)
    ROWS = NS2 * T
    RW = M + 1
    SPARE = NB
    CB = 14
    NC = NB // CB
    assert NC * CB == NB
    WC = F + 2 * M
    FG = 4
    NG = -(-NB // FG)

    rows = nc.dram_tensor("edge_rows", (ROWS, RW), f32, kind="Internal").ap()
    b_parts = nc.dram_tensor("b_parts", ((NB + 1) * P, 3 * M), bf16, kind="Internal").ap()
    b_rows = nc.dram_tensor("b_rows", (NB * P, M), f32, kind="Internal").ap()
    bucket_dram = nc.dram_tensor("bucket_of", (1, P * 8), i32, kind="Internal").ap()

    ctx = ExitStack()
    with ctx:
        def sb(name, shape, dt, where=ctx):
            return where.enter_context(nc.sbuf_tensor(name, shape, dt))

        def sem(name):
            return ctx.enter_context(nc.semaphore(name))

        psum = ctx.enter_context(nc.psum_tensor("psum", [P, 8, 512], f32))
        psumb = psum[:, :, :].bitcast(bf16)

        ident = sb("ident", [P, P], bf16)
        identf = sb("identf", [P, P], f32)
        ones = sb("ones", [P, P], bf16)
        onesf = sb("onesf", [P, P], f32)
        upper = sb("upper", [P, P], bf16)
        iota_i = sb("iota_i", [P, P], i32)
        part_i = sb("part_i", [P, 1], i32)
        sidx_i = sb("sidx_i", [P, 8], i32)
        iota = sb("iota", [P, P], bf16)
        iotaf = sb("iotaf", [P, P], f32)
        partf = sb("partf", [P, 1], f32)
        sidx = sb("sidx", [P, 8], f32)
        eps = sb("eps", [P, 1], f32)
        filler = sb("filler", [P, 1243], f32)
        assert (ROWS * RW) % (P * 1243) == 0
        wcat = sb("wcat", [P, WC], f32)
        bias = sb("bias", [P, WC], f32)
        w_ef = sb("w_ef", [P, 2 * M], f32)
        w_sum = sb("w_sum", [P, FG, F], f32)
        hi_col = sb("hi_col", [P, SB * P, J], bf16)
        lo_col = sb("lo_col", [P, SB * P, J], bf16)
        dst_col = sb("dst_col", [P, SB * P, J], i32)
        rel_row = sb("rel_row", [P, SB, T], bf16)
        base = sb("base", [P, NB], f32)
        match = sb("match", [P, 1], f32)
        general_i = sb("general_i", [P, 1], i32)
        bucket_row = sb("bucket_row", [1, P * 8], i32)
        a_tab = sb("a_tab", [P, NB + 1, 3, M], bf16)
        ypart = sb("ypart", [P, NB, F], f32)

        consts, cast = sem("consts"), sem("cast")
        weights_in, idx_in, idx_clear = sem("weights_in"), sem("idx_in"), sem("idx_clear")
        w_clear = sem("w_clear")
        filled = sem("filled")
        dve_e, cols_t, cols_out = sem("dve_e"), sem("cols_t"), sem("cols_out")
        idx_rows, viol_ready, counted, buckets_ready = sem("idx_rows"), sem("viol_ready"), sem("counted"), sem("buckets_ready")
        dcols_out, count_mm, flag_mm = sem("dcols_out"), sem("count_mm"), sem("flag_mm")
        bucket_out, bucket_in = sem("bucket_out"), sem("bucket_in")
        with ExitStack() as tmp:
            src_row = sb("src_row", [P, SB, T], i32, tmp)
            dst_row = sb("dst_row", [P, SB, T], i32, tmp)
            t1 = sb("t1", [P, SB, T], i32, tmp)
            t2 = sb("t2", [P, SB, T], i32, tmp)
            hi_row = sb("hi_row", [P, SB, T], bf16, tmp)
            lo_row = sb("lo_row", [P, SB, T], bf16, tmp)
            spans = sb("spans", [P, 4, SB], f32, tmp)
            viol = sb("viol", [P, 1], f32, tmp)
            violb = sb("violb", [P, 1], bf16, tmp)
            part_counts = sb("part_counts", [P, NB], f32, tmp)
            c_f = sb("c_f", [P, 3, NB], f32, tmp)
            c_i = sb("c_i", [P, 2, NB], i32, tmp)
            cmp = sb("cmp", [P, 8, NB], f32, tmp)
            bk_f = sb("bk_f", [P, 8], f32, tmp)
            bk_i = sb("bk_i", [P, 8], i32, tmp)
            REST = NS - 1 - (SB - 1) * P
            block = tmp.enter_context(nc.Block())

            @block.sync
            def _(sp):
                full = (SB - 1) * P * T
                for row, arr in ((src_row, src), (dst_row, dst)):
                    sp.dma_start(row[:, 0:SB - 1, :], arr[0:full].rearrange("(b s e) -> s b e", s=P, e=T)).then_inc(idx_in, 16)
                sp.wait_ge(idx_clear, 2)
                for row, arr in ((src_row, src), (dst_row, dst)):
                    sp.dma_start(row[0:REST, SB - 1, :], arr[full:full + REST * T].rearrange("(s e) -> s e", e=T)).then_inc(idx_in, 16)
                    sp.dma_start(row[REST:REST + 1, SB - 1, :], arr[LAST0:E].rearrange("(s e) -> s e", e=T)).then_inc(idx_in, 16)
                sp.wait_ge(buckets_ready, 1)
                sp.dma_start(bucket_dram.rearrange("o (p c) -> (o p) c", c=8), bk_i[:, :]).then_inc(bucket_out, 16)
                sp.wait_ge(bucket_out, 16)
                sp.dma_start(bucket_row[:, :], bucket_dram).then_inc(bucket_in, 16)
                sp.wait_ge(bucket_in, 16)

            @block.gpsimd
            def _(pool):
                pool.memset(src_row[:, SB - 1, :], 0).then_inc(idx_clear, 1)
                pool.memset(dst_row[:, SB - 1, :], 0).then_inc(idx_clear, 1)
                pool.memset(filler[:, :], -1.0).then_inc(consts, 1)
                pool.memset(w_ef[:, :], 0.0).then_inc(w_clear, 1)
                pool.memset(w_sum[:, :, :], 0.0).then_inc(w_clear, 1)
                pool.memset(bias[:, F:F + M], 0.0).then_inc(w_clear, 1)
                pool.memset(ones[:, :], 1.0).then_inc(consts, 1)
                pool.memset(onesf[:, :], 1.0).then_inc(consts, 1)
                pool.memset(eps[:, :], 1e-5).then_inc(consts, 1)
                pool.memset(ident[:, :], 0.0).then_inc(consts, 1)
                pool.memset(identf[:, :], 0.0).then_inc(consts, 1)
                pool.iota(iota_i[:, :], pattern=[[1, P]], base=0, channel_multiplier=0).then_inc(consts, 1)
                pool.iota(part_i[:, :], pattern=[[0, 1]], base=0, channel_multiplier=1).then_inc(consts, 1)
                pool.iota(sidx_i[:, :], pattern=[[1, 8]], base=0, channel_multiplier=8).then_inc(consts, 1)
                pool.wait_ge(consts, 9)
                for m in (ident, identf):
                    pool.affine_select(out=m[:, :], in_=m[:, :], compare_op=ALU.not_equal, fill=1.0, base=0,
                                       pattern=[[-1, P]], channel_multiplier=1).then_inc(consts, 1)
                pool.affine_select(out=upper[:, :], in_=ones[:, :], compare_op=ALU.is_gt, fill=0.0, base=0,
                                   pattern=[[1, P]], channel_multiplier=-1).then_inc(consts, 1)

            @block.vector
            def _(dve):
                n = [0]

                def link(ins, signal=None):
                    if signal is not None:
                        ins.then_inc(signal, 1)
                        dve.wait_ge(signal, 1)
                        return
                    n[0] += 1
                    ins.then_inc(dve_e, 1)
                    dve.wait_ge(dve_e, n[0])

                v = nc.vector
                dve.wait_ge(consts, 12)
                v.tensor_copy(iota[:, :], iota_i[:, :]).then_inc(cast, 1)
                v.tensor_copy(iotaf[:, :], iota_i[:, :]).then_inc(cast, 1)
                v.tensor_copy(partf[:, :], part_i[:, :]).then_inc(cast, 1)
                v.tensor_copy(sidx[:, :], sidx_i[:, :]).then_inc(cast, 1)
                dve.wait_ge(idx_in, 16 * 6)
                link(v.tensor_single_scalar(t1[:, :, :], src_row[:, :, :], P.bit_length() - 1, ALU.arith_shift_right))
                link(v.tensor_single_scalar(t2[:, :, :], src_row[:, :, :], P - 1, ALU.bitwise_and))
                link(v.tensor_copy(hi_row[:, :, :], t1[:, :, :]))
                link(v.tensor_copy(lo_row[:, :, :], t2[:, :, :]))
                dst_f, rel = t1[:, :, :].bitcast(f32), t2[:, :, :].bitcast(f32)
                link(v.tensor_copy(dst_f, dst_row[:, :, :]), idx_rows)
                link(v.tensor_tensor(out=rel, in0=dst_f, in1=dst_f[:, :, 0:1].broadcast_to([P, SB, T]), op=ALU.subtract))
                for b in range(SB):
                    link(v.tensor_copy(rel_row[:, b, :].rearrange("s (j p) -> s p j", j=J),
                                       rel[:, b, :].rearrange("s (p j) -> s p j", j=J)))
                link(v.tensor_reduce(out=spans[:, 0, :], in_=rel, op=ALU.max, axis=AX))
                link(v.tensor_reduce(out=spans[:, 1, :], in_=rel, op=ALU.min, axis=AX))
                link(v.tensor_single_scalar(spans[:, 2, :], spans[:, 0, :], float(P), ALU.is_ge))
                link(v.tensor_single_scalar(spans[:, 3, :], spans[:, 1, :], 0.0, ALU.is_lt))
                link(v.tensor_reduce(out=viol[:, :], in_=spans[:, 2:4, :].rearrange("p a b -> p (a b)"), op=ALU.add, axis=AX))
                link(v.tensor_copy(violb[:, :], viol[:, :]), viol_ready)
                for b in range(SB):
                    dve.wait_ge(cols_t, b + 1)
                    v.tensor_copy(dst_col[:, b * P:(b + 1) * P, :],
                                  psum[:, 4 + b % 2, :].rearrange("p (j s) -> p s j", j=J)).then_inc(dcols_out, 1)
                dve.wait_ge(flag_mm, 1)
                link(v.tensor_scalar(viol[:, :], psum[:, 6, 0:1], 1.0, None, ALU.min))
                link(v.tensor_copy(general_i[:, :], viol[:, :]))
                link(v.scalar_tensor_tensor(out=match[:, :], in0=viol[:, :], scalar=0.5, in1=partf[:, :], op0=ALU.mult, op1=ALU.add))
                dve.wait_ge(cols_out, 2 * SB)
                link(v.memset(hi_col[0:SEEN, NS - 1, :], float(P - 1)))
                flat = hi_col[:, 0:NS, :].rearrange("p s j -> p (s j)")
                junk = hi_row[:, :, :].rearrange("p b e -> p (b e)")[:, 0:NS * J]
                with dve.Fori(0, NB) as h:
                    v.tensor_scalar(junk, flat, iotaf[:, ds(h, 1)], 0.0, ALU.is_equal, ALU.add,
                                    accum_out=part_counts[:, ds(h, 1)]).then_inc(counted, 1)
                    dve.wait_ge(counted, h + 1)
                dve.wait_ge(count_mm, 1)
                link(v.tensor_scalar(c_f[:, 0, :], psum[:, 7, 0:NB], float(T - 1), None, ALU.add))
                link(v.tensor_copy(c_i[:, 0, :], c_f[:, 0, :]))
                link(v.tensor_single_scalar(c_i[:, 1, :], c_i[:, 0, :], T.bit_length() - 1, ALU.arith_shift_right))
                link(v.tensor_copy(c_f[:, 0, :], c_i[:, 1, :]))
                link(v.tensor_tensor_scan(out=c_f[:, 1, :], data0=onesf[:, 0:NB], data1=c_f[:, 0, :], initial=0.0,
                                          op0=ALU.mult, op1=ALU.add))
                link(v.tensor_tensor(out=cmp[:, :, :], in0=c_f[:, 1:2, :].broadcast_to([P, 8, NB]),
                                     in1=sidx[:, :].unsqueeze(2).broadcast_to([P, 8, NB]), op=ALU.is_le))
                link(v.tensor_tensor(out=c_f[:, 2, :], in0=c_f[:, 1, :], in1=c_f[:, 0, :], op=ALU.subtract))
                link(v.tensor_scalar(base[:, :], c_f[:, 2, :], float(T), None, ALU.mult))
                link(v.tensor_reduce(out=bk_f[:, :], in_=cmp[:, :, :], op=ALU.add, axis=AX))
                link(v.tensor_copy(bk_i[:, :], bk_f[:, :]), buckets_ready)

            @block.tensor
            def _(pe):
                pe.wait_ge(consts, 12)
                pe.wait_ge(idx_rows, 1)
                for b in range(SB):
                    if b >= 2:
                        pe.wait_ge(cols_out, 2 * (b - 1))
                        pe.wait_ge(dcols_out, b - 1)
                    for bank, row, idn in ((0, hi_row, ident), (2, lo_row, ident), (4, t1[:, :, :].bitcast(f32), identf)):
                        for j in range(J):
                            out = psum[:, 4 + b % 2, j * P:(j + 1) * P] if bank == 4 else psumb[:, bank + b % 2, j * P:(j + 1) * P]
                            last = nc.tensor.transpose(out, row[:, b, :].rearrange("s (p j) -> s j p", j=J)[:, j, :], idn[:, :])
                    last.then_inc(cols_t, 1)
                pe.wait_ge(viol_ready, 1)
                nc.tensor.matmul(psum[:, 6, 0:1], ones[:, :], violb[:, :], start=True, stop=True).then_inc(flag_mm, 1)
                pe.wait_ge(counted, NB)
                nc.tensor.matmul(psum[:, 7, 0:NB], onesf[:, :], part_counts[:, :], start=True, stop=True).then_inc(count_mm, 1)

            @block.scalar
            def _(act):
                act.wait_ge(w_clear, 3)
                act.dma_start(wcat[:, 0:F], w_node[0:F, :]).then_inc(weights_in, 16)
                act.dma_start(wcat[:, F:F + M], w_edge[0:F, :]).then_inc(weights_in, 16)
                act.dma_start(wcat[:, F + M:WC], w_edge[F:2 * F, :]).then_inc(weights_in, 16)
                for q in range(2):
                    act.dma_start(w_ef[q * FE:(q + 1) * FE, q * M:(q + 1) * M], w_edge[2 * F:2 * F + FE, :]).then_inc(weights_in, 16)
                for q in range(FG):
                    act.dma_start(w_sum[q * M:(q + 1) * M, q, :], w_node[F:F + M, :]).then_inc(weights_in, 16)
                act.dma_start(bias[:, 0:F], b_node.unsqueeze(0).broadcast_to([P, F])).then_inc(weights_in, 16)
                act.dma_start(bias[:, F + M:WC], b_edge.unsqueeze(0).broadcast_to([P, M])).then_inc(weights_in, 16)
                act.wait_ge(consts, 1)
                reps = ROWS * RW // (P * 1243)
                act.dma_start(rows.rearrange("r c -> (r c)").rearrange("(p a c) -> p a c", p=P, c=1243),
                              filler[:, :].unsqueeze(1).broadcast_to([P, reps, 1243])).then_inc(filled, 16)
                for b in range(SB):
                    act.wait_ge(cols_t, b + 1)
                    for bank, col in ((0, hi_col), (2, lo_col)):
                        nc.scalar.copy(col[:, b * P:(b + 1) * P, :],
                                       psumb[:, bank + b % 2, 0:T].rearrange("p (j s) -> p s j", j=J)).then_inc(cols_out, 1)

        x_in = [sem("x_in0"), sem("x_in1")]
        row_sum, mean, centred, sq_done = sem("row_sum"), sem("mean"), sem("centred"), sem("sq_done")
        sq_sum, std_done, inv_std = sem("sq_sum"), sem("std_done"), sem("inv_std")
        h_ready, ht_t, ht_out = sem("h_ready"), sem("ht_t"), sem("ht_out")
        node_mm, node_out = sem("node_mm"), sem("node_out")
        part_h, part_r, part_m, part_l = sem("part_h"), sem("part_r"), sem("part_m"), sem("part_l")
        b_out, spare_clear, spare_out, tabs_done = sem("b_out"), sem("spare_clear"), sem("spare_out"), sem("tabs_done")
        with ExitStack() as tmp:
            xb = sb("xb", [P, 2, CB, F], f32, tmp)
            xc = sb("xc", [P, CB, F], f32, tmp)
            sq = sb("sq", [P, CB, F], f32, tmp)
            hn = sb("hn", [P, CB, F], f32, tmp)
            ht = sb("ht", [P, 2, P], f32, tmp)
            stat = sb("stat", [P, 5, CB], f32, tmp)
            ab = sb("ab", [P, CB, 2 * M], f32, tmp)
            rest = sb("rest", [P, CB, 2 * M], f32, tmp)
            abp = sb("abp", [P, 3, CB, 2 * M], bf16, tmp)
            bst = sb("bst", [P, CB, 3, M], bf16, tmp)
            block = tmp.enter_context(nc.Block())

            @block.sync
            def _(sp):
                def load(c, k, whole):
                    r0 = c * (CB * P)
                    sp.dma_start(xb[:, k, 0:CB - 1, :],
                                 x[ds(r0, (CB - 1) * P), :].rearrange("(b p) f -> p b f", p=P)).then_inc(x_in[k], 16)
                    n = P if whole else NTAIL
                    sp.dma_start(xb[0:n, k, CB - 1, :], x[ds(r0 + (CB - 1) * P, n), :]).then_inc(x_in[k], 16)

                def store(c):
                    sp.wait_ge(tabs_done, 4 * (c + 1))
                    sp.dma_start(b_parts[ds(c * (CB * P), CB * P), :].rearrange("(b p) m -> p b m", p=P),
                                 bst[:, :, :, :].rearrange("p b t m -> p b (t m)")).then_inc(b_out, 16)
                    sp.dma_start(b_rows[ds(c * (CB * P), CB * P), :].rearrange("(b p) m -> p b m", p=P),
                                 ab[:, :, M:2 * M]).then_inc(b_out, 16)

                for c in range(NC):
                    if c >= 2:
                        sp.wait_ge(centred, c - 1)
                    load(c, c % 2, c < NC - 1)
                    if c >= 1:
                        store(c - 1)
                store(NC - 1)
                sp.wait_ge(b_out, 32 * NC)
            @block.gpsimd
            def _(pool):
                pool.memset(a_tab[:, NB, :, :], 0.0).then_inc(spare_clear, 1)
                pool.memset(bst[:, 0, :, :], 0.0).then_inc(spare_clear, 1)
                pool.wait_ge(spare_clear, 2)
                pool.dma_start(b_parts[NB * P:(NB + 1) * P, :], bst[:, 0, :, :].rearrange("p t m -> p (t m)")).then_inc(spare_out, 16)
                pool.wait_ge(spare_out, 16)

            @block.vector
            def _(dve):
                v = nc.vector
                dve.wait_ge(spare_out, 16)
                with dve.Fori(0, NC) as c:
                    xs = xb[:, ds(c % 2, 1), :, :].rearrange("p o b f -> p (o b) f")

                    def done(ins, signal):
                        ins.then_inc(signal, 1)
                        dve.wait_ge(signal, c + 1)

                    def bc(i):
                        return stat[:, i, :].unsqueeze(2).broadcast_to([P, CB, F])

                    dve.wait_ge(x_in[0], 32 * ((c + 2) // 2))
                    dve.wait_ge(x_in[1], 32 * ((c + 1) // 2))
                    done(v.tensor_reduce(out=stat[:, 0, :], in_=xs, op=ALU.add, axis=AX), row_sum)
                    done(v.tensor_scalar(stat[:, 1, :], stat[:, 0, :], 1.0 / F, None, ALU.mult), mean)
                    done(v.tensor_tensor(out=xc[:, :, :], in0=xs, in1=bc(1), op=ALU.subtract), centred)
                    dve.wait_ge(sq_done, c + 1)
                    done(v.tensor_reduce(out=stat[:, 2, :], in_=sq[:, :, :], op=ALU.add, axis=AX), sq_sum)
                    dve.wait_ge(std_done, c + 1)
                    done(v.reciprocal(stat[:, 4, :], stat[:, 3, :]), inv_std)
                    done(v.tensor_tensor(out=hn[:, :, :], in0=xc[:, :, :], in1=bc(4), op=ALU.mult), h_ready)
                    for b in range(CB):
                        dve.wait_ge(node_mm, c * CB + (b + 1))
                        bank = 2 + b % 2
                        v.tensor_tensor(out=ypart[:, ds(c * CB + b, 1), :].rearrange("p o f -> p (o f)"),
                                        in0=psum[:, bank, 0:F], in1=bias[:, 0:F], op=ALU.add)
                        if b == 0:
                            dve.wait_ge(b_out, 32 * c)
                        v.tensor_tensor(out=ab[:, b, :], in0=psum[:, bank, F:WC], in1=bias[:, F:WC], op=ALU.add)\
                            .then_inc(node_out, 1)
                    dve.wait_ge(part_h, c + 1)
                    done(v.tensor_tensor(out=rest[:, :, :], in0=ab[:, :, :], in1=abp[:, 0, :, :], op=ALU.subtract), part_r)
                    dve.wait_ge(part_m, c + 1)
                    done(v.tensor_tensor(out=abp[:, 2, :, :], in0=rest[:, :, :], in1=abp[:, 1, :, :], op=ALU.subtract), part_l)
                    for t in range(3):
                        v.tensor_copy(bst[:, :, t, :], abp[:, t, :, M:2 * M])
                        last = v.tensor_copy(a_tab[:, ds(c * CB, CB), t, :], abp[:, t, :, 0:M])
                    last.then_inc(tabs_done, 4)
                    dve.wait_ge(tabs_done, 4 * (c + 1))

            @block.tensor
            def _(pe):
                pe.wait_ge(weights_in, 16 * (5 + FG + 2))
                with pe.Fori(0, NC) as c:
                    pe.wait_ge(h_ready, c + 1)

                    def transpose(b):
                        if b >= 2:
                            pe.wait_ge(ht_out, c * CB + (b - 1))
                        nc.tensor.transpose(psum[:, b % 2, 0:P], hn[:, b, :], identf[:, :]).then_inc(ht_t, 1)

                    transpose(0)
                    for b in range(CB):
                        if b + 1 < CB:
                            transpose(b + 1)
                        pe.wait_ge(ht_out, c * CB + (b + 1))
                        if b >= 2:
                            pe.wait_ge(node_out, c * CB + (b - 1))
                        nc.tensor.matmul(psum[:, 2 + b % 2, 0:WC], ht[:, b % 2, :], wcat[:, :], start=True, stop=True)\
                            .then_inc(node_mm, 1)
                    pe.wait_ge(node_out, (c + 1) * CB)

            @block.scalar
            def _(act):
                a = nc.scalar
                with act.Fori(0, NC) as c:
                    act.wait_ge(centred, c + 1)
                    a.activation(sq[:, :, :], xc[:, :, :], ACT.Square).then_inc(sq_done, 1)
                    act.wait_ge(sq_sum, c + 1)
                    a.activation(stat[:, 3, :], stat[:, 2, :], ACT.Sqrt, bias=eps[:, :], scale=1.0 / F).then_inc(std_done, 1)
                    for b in range(CB):
                        act.wait_ge(ht_t, c * CB + (b + 1))
                        if b >= 2:
                            act.wait_ge(node_mm, c * CB + (b - 1))
                        a.activation(ht[:, b % 2, :], psum[:, b % 2, 0:P], ACT.Relu).then_inc(ht_out, 1)
                    act.wait_ge(node_out, (c + 1) * CB)
                    a.copy(abp[:, 0, :, :], ab[:, :, :]).then_inc(part_h, 1)
                    act.wait_ge(part_r, c + 1)
                    a.copy(abp[:, 1, :, :], rest[:, :, :]).then_inc(part_m, 1)

        ef_in = [sem("ef_in0"), sem("ef_in1")]
        bw_in = [sem("bw_in0"), sem("bw_in1")]
        scattered = [sem("scattered0"), sem("scattered1")]
        gathered_dma, gathered, gidx_ready = sem("gathered_dma"), sem("gathered"), sem("gidx_ready")
        g_clear, pool_turns = sem("g_clear"), sem("pool_turns")
        ef_t, ef_out, rel_bc = sem("ef_t"), sem("ef_out"), sem("rel_bc")
        window, onehot, ranks, pre = sem("window"), sem("onehot"), sem("ranks"), sem("pre")
        dve_p, pos_ready, rec_ready, lo_ready = sem("dve_p"), sem("pos_ready"), sem("rec_ready"), sem("lo_ready")
        ranks_read, tail_pos = sem("ranks_read"), sem("tail_pos")
        with ExitStack() as tmp:
            eft_in = sb("eft_in", [P, 2, J, FE], f32, tmp)
            eft = sb("eft", [P, 2, 2 * P], f32, tmp)
            bwin = sb("bwin", [P, 2, 3, M], bf16, tmp)
            win = sb("win", [P, 2, T], bf16, tmp)
            hot = sb("hot", [P, 2, J, NB], bf16, tmp)
            s1 = sb("s1", [P, J, NB], f32, tmp)
            s2 = sb("s2", [P, J, NB], f32, tmp)
            pos_f = sb("pos_f", [P, J], f32, tmp)
            pos = sb("pos", [P, 2, J], i32, tmp)
            rec = sb("rec", [P, 2, J, RW], f32, tmp)
            gat = sb("gat", [P, 2, J, M], f32, tmp)
            gidx = sb("gidx", [P, 2, J], i32, tmp)
            block = tmp.enter_context(nc.Block())

            def in_pairs(eng, step):
                for k in range(2):
                    step(0, k)
                with eng.Fori(1, NS // 2 - 1) as i:
                    for k in range(2):
                        step(i, k)
                for k in range(2):
                    step(NS // 2 - 1, k)

            def after(i, k, n=1):
                return i + (k + n) // 2, (k + n) % 2

            def start_of(i, k):
                return LAST0 if isinstance(i, int) and 2 * i + k == NS - 1 else (2 * i + k) * T

            def exists(i, k):
                return not isinstance(i, int) or 0 <= 2 * i + k < NS

            @block.sync
            def _(sp):
                def step(i, k):
                    t, e0 = 2 * i + k, start_of(i, k)
                    later = not (isinstance(i, int) and i == 0)
                    if later:
                        sp.wait_ge(ef_t, t - 1)
                    sp.dma_start(eft_in[:, k, :, :].rearrange("p j f -> p (j f)"),
                                 ef[ds(e0, T), :].rearrange("(p j) f -> p (j f)", j=J)).then_inc(ef_in[k], 16)
                    first = sp.value_load(dst[ds(e0, 1)].rearrange("(a b) -> a b", a=1), min_val=0, max_val=N - 1)
                    if later:
                        sp.wait_ge(pre, t - 1)
                    sp.dma_start(bwin[:, k, :, :].rearrange("p t m -> p (t m)"), b_parts[ds(first, P), :]).then_inc(bw_in[k], 16)
                in_pairs(sp, step)

            @block.gpsimd
            def _(pool):
                pool.memset(gat[:, :, :, :], 0.0).then_inc(g_clear, 1)
                pool.wait_ge(g_clear, 1)
                pool.wait_ge(filled, 16)

                def step(i, k, general):
                    t = 2 * i + k
                    later = not (isinstance(i, int) and i == 0)
                    if general:
                        if later:
                            pool.wait_ge(rec_ready, t - 1)
                        pool.tensor_copy(gidx[:, k, :], dst_col[:, ds(t, 1), :].rearrange("p o j -> p (o j)")).then_inc(gidx_ready, 1)
                        pool.wait_ge(gidx_ready, t + 1)
                        pool.sem_inc(pool_turns, 1)
                        for j in range(J):
                            pool.indirect_dma_start(out=gat[:, k, j, :], out_offset=None, in_=b_rows[:, :],
                                                    in_offset=bass.IndirectOffsetOnAxis(ap=gidx[:, k, j:j + 1], axis=0))\
                                .then_inc(gathered_dma, 16)
                        pool.wait_ge(gathered_dma, 16 * J * (t + 1))
                        pool.sem_inc(gathered, 1)
                    pool.wait_ge(pos_ready, t + 1)
                    pool.wait_ge(lo_ready, t + 1)
                    pool.wait_ge(rec_ready, t + 1)
                    pool.sem_inc(pool_turns, 1)
                    for j in range(J):
                        pool.indirect_dma_start(out=rows[:, :], out_offset=bass.IndirectOffsetOnAxis(ap=pos[:, k, j:j + 1], axis=0),
                                                in_=rec[:, k, j, :], in_offset=None,
                                                bounds_check=ROWS - 1, oob_is_err=False).then_inc(scattered[k], 16)

                flag = pool.value_load(general_i[0:1, 0:1], min_val=0, max_val=1)
                with pool.If(flag != 0):
                    in_pairs(pool, lambda i, k: step(i, k, True))
                with pool.Else():
                    pool.sem_inc(gathered, NS)
                    in_pairs(pool, lambda i, k: step(i, k, False))
                for k in range(2):
                    pool.wait_ge(scattered[k], 16 * J * (NS // 2))

            @block.tensor
            def _(pe):
                te = nc.tensor

                def spread(i, k):
                    if not exists(i, k):
                        return
                    t = 2 * i + k
                    later = not (isinstance(i, int) and i == 0)
                    if later:
                        pe.wait_ge(ef_out, t - 1)
                    pe.wait_ge(ef_in[k], 16 * (i + 1))
                    for q in range(2):
                        last = te.transpose(psum[:, k, q * P:(q + 1) * P],
                                            eft_in[:, k, 2 * q:2 * q + 2, :].rearrange("p j f -> p (j f)"), identf[:, :])
                    last.then_inc(ef_t, 1)
                    if later:
                        pe.wait_ge(window, t - 1)
                    te.matmul(psum[:, 2 + k, :], ident[:, ds(t % P, 1)].broadcast_to([P, P]),
                              rel_row[:, ds(t // P, 1), :].rearrange("s o e -> s (o e)"), start=True, stop=True).then_inc(rel_bc, 1)

                def step(i, k):
                    t = 2 * i + k
                    later = not (isinstance(i, int) and i == 0)
                    spread(*after(i, k))
                    cum = psum[:, 4 + k, :]
                    h = hot[:, k, :, :].rearrange("p j b -> p (j b)")
                    pe.wait_ge(onehot, t + 1)
                    if later:
                        pe.wait_ge(ranks_read, t - 1)
                    te.matmul(cum[:, 0:J * NB], upper[:, :], h, start=True, stop=False)
                    te.matmul(cum[:, J * NB:(J + 1) * NB], ones[:, :], h[:, (J - 1) * NB:], start=False, stop=False)
                    te.matmul(cum[:, NB:J * NB], ones[:, :], h[:, 0:(J - 1) * NB], start=False, stop=False)
                    for d in range(2, J + 1):
                        last = te.matmul(cum[:, d * NB:(J + 1) * NB], ones[:, :], h[:, 0:(J + 1 - d) * NB], start=False, stop=d == J)
                    last.then_inc(ranks, 1)
                    out = psum[:, 6 + k, 0:J * M]
                    pe.wait_ge(ef_out, t + 1)
                    if later:
                        pe.wait_ge(rec_ready, t - 1)
                    for q in range(2):
                        te.matmul(out[:, q * 2 * M:(q + 1) * 2 * M], eft[:, k, q * P:(q + 1) * P], w_ef[:, :], start=q == 0, stop=False)
                    pe.wait_ge(window, t + 1)
                    pe.wait_ge(bw_in[k], 16 * (i + 1))
                    for j in range(J):
                        for part in range(3):
                            last = te.matmul(out[:, j * M:(j + 1) * M], win[:, k, j * P:(j + 1) * P], bwin[:, k, part, :],
                                             start=False, stop=j == J - 1 and part == 2)
                    last.then_inc(pre, 1)

                spread(0, 0)
                in_pairs(pe, step)

            @block.scalar
            def _(act):
                def step(i, k):
                    t = 2 * i + k
                    later = not (isinstance(i, int) and i == 0)
                    act.wait_ge(ef_t, t + 1)
                    if later:
                        act.wait_ge(pre, t - 1)
                    nc.scalar.copy(eft[:, k, :], psum[:, k, 0:2 * P]).then_inc(ef_out, 1)
                    if later:
                        act.wait_ge(scattered[k], 16 * J * i)
                    nc.scalar.copy(rec[:, k, :, M:RW], lo_col[:, ds(t, 1), :].rearrange("p o j -> p j o")).then_inc(lo_ready, 1)
                in_pairs(act, step)

            @block.vector
            def _(dve):
                v = nc.vector

                def onehots(i, k):
                    if not exists(i, k):
                        return
                    t = 2 * i + k
                    later = not (isinstance(i, int) and i == 0)
                    dve.wait_ge(rel_bc, t + 1)
                    if later:
                        dve.wait_ge(pre, t - 1)
                    v.tensor_scalar(win[:, k, :], psum[:, 2 + k, :], match[:, 0:1], None, ALU.is_equal).then_inc(window, 1)
                    if later:
                        dve.wait_ge(ranks, t - 1)
                        dve.wait_ge(pos_ready, t - 1)
                    v.tensor_tensor(out=hot[:, k, :, :], in0=iota[:, 0:NB].unsqueeze(1).broadcast_to([P, J, NB]),
                                    in1=hi_col[:, ds(t, 1), :].rearrange("p o j -> p j o").broadcast_to([P, J, NB]),
                                    op=ALU.is_equal).then_inc(onehot, 1)

                def step(i, k):
                    t = 2 * i + k
                    later = not (isinstance(i, int) and i == 0)
                    onehots(*after(i, k))
                    cum = psum[:, 4 + k, :]
                    dve.wait_ge(ranks, t + 1)
                    if later or k:
                        dve.wait_ge(ranks_read, t)
                    v.tensor_tensor(out=s1[:, :, :], in0=cum[:, 0:J * NB].rearrange("p (j b) -> p j b", j=J),
                                    in1=base[:, :].unsqueeze(1).broadcast_to([P, J, NB]), op=ALU.add).then_inc(dve_p, 1)
                    dve.wait_ge(dve_p, 3 * t + 1)
                    v.tensor_tensor(out=base[:, :], in0=base[:, :], in1=cum[:, J * NB:(J + 1) * NB], op=ALU.add).then_inc(ranks_read, 1)
                    v.tensor_tensor(out=s2[:, :, :], in0=s1[:, :, :], in1=hot[:, k, :, :], op=ALU.mult).then_inc(dve_p, 1)
                    dve.wait_ge(pre, t + 1)
                    dve.wait_ge(gathered, t + 1)
                    if later:
                        dve.wait_ge(scattered[k], 16 * J * i)
                    v.tensor_tensor(out=rec[:, k, :, 0:M], in0=psum[:, 6 + k, 0:J * M].rearrange("p (j m) -> p j m", j=J),
                                    in1=gat[:, k, :, :], op=ALU.add).then_inc(rec_ready, 1)
                    dve.wait_ge(dve_p, 3 * t + 2)
                    v.tensor_reduce(out=pos_f[:, :], in_=s2[:, :, :], op=ALU.add, axis=AX).then_inc(dve_p, 1)
                    dve.wait_ge(dve_p, 3 * t + 3)
                    tail = isinstance(i, int) and t == NS - 1
                    ins = v.tensor_copy(pos[:, k, :], pos_f[:, :])
                    if tail:
                        ins.then_inc(tail_pos, 1)
                        dve.wait_ge(tail_pos, 1)
                        ins = v.memset(pos[0:SEEN, k, :], ROWS)
                    ins.then_inc(pos_ready, 1)

                onehots(0, 0)
                in_pairs(dve, step)

        acc = sb("acc", [P, FG * NG, M], f32)
        assert FG * NG > NB
        GS = 4
        NGR = NS2 // GS
        rows_in = [sem("rows_in0"), sem("rows_in1")]
        acc_clear = sem("acc_clear")
        lo_hot, lo_hot_t, lo_hot_out = sem("lo_hot"), sem("lo_hot_t"), sem("lo_hot_out")
        a_mm, summed, msg_h, msg_r, msg_m, msg_l = sem("a_mm"), sem("summed"), sem("msg_h"), sem("msg_r"), sem("msg_m"), sem("msg_l")
        sum_mm, sum_added = sem("sum_mm"), sem("sum_added")
        with ExitStack() as tmp:
            rec2 = sb("rec2", [P, 2, GS, J, RW], f32, tmp)
            lhot = sb("lhot", [P, GS, J, P], bf16, tmp)
            lhot_t = sb("lhot_t", [P, 2, J, P], bf16, tmp)
            msg = sb("msg", [P, 2, J, M], f32, tmp)
            msgr = sb("msgr", [P, 2, J, M], f32, tmp)
            msgp = sb("msgp", [P, 2, 3, J, M], bf16, tmp)
            block = tmp.enter_context(nc.Block())

            def shift(g, k, n):
                return g + (k + n) // GS, (k + n) % GS

            def inside(g, k):
                return not isinstance(g, int) or 0 <= GS * g + k < NS2

            def from_(g, k, n):
                return not isinstance(g, int) or GS * g + k >= n

            def in_groups(eng, step):
                for g in (-1, 0):
                    for k in range(GS):
                        step(g, k)
                with eng.Fori(1, NGR - 1) as g:
                    for k in range(GS):
                        step(g, k)
                for g in (NGR - 1, NGR):
                    for k in range(GS):
                        step(g, k)

            @block.sync
            def _(sp):
                def load(g, q, later):
                    if later:
                        sp.wait_ge(summed, GS * (g - 1))
                    sp.dma_start(rec2[:, q, :, :, :].rearrange("p s j w -> p s (j w)"),
                                 rows[ds(g * (GS * T), GS * T), :].rearrange("(s p j) w -> p s (j w)", s=GS, j=J))\
                        .then_inc(rows_in[q], 16)
                for q in range(2):
                    load(q, q, False)
                with sp.Fori(1, NGR // 2) as i:
                    for q in range(2):
                        load(2 * i + q, q, True)

            @block.gpsimd
            def _(pool):
                pool.memset(acc[:, :, :], 0.0).then_inc(acc_clear, 1)

            @block.tensor
            def _(pe):
                te = nc.tensor

                def turn(g, k):
                    if not inside(g, k):
                        return
                    s = GS * g + k
                    pe.wait_ge(lo_hot, s + 1)
                    if from_(g, k, 2):
                        pe.wait_ge(lo_hot_out, s - 1)
                    for j in range(J):
                        last = te.transpose(psumb[:, k % 2, j * P:(j + 1) * P], lhot[:, k, j, :], ident[:, :])
                    last.then_inc(lo_hot_t, 1)

                def add_a(g, k):
                    if not inside(g, k):
                        return
                    s = GS * g + k
                    bucket = pe.value_load(bucket_row[0:1, ds(s, 1)], min_val=0, max_val=SPARE)
                    pe.wait_ge(lo_hot_out, s + 1)
                    if from_(g, k, 2):
                        pe.wait_ge(summed, s - 1)
                    for j in range(J):
                        for part in range(3):
                            last = te.matmul(psum[:, 2 + k % 2, j * M:(j + 1) * M], lhot_t[:, k % 2, j, :],
                                             a_tab[:, ds(bucket, 1), part, :].rearrange("p o m -> p (o m)"),
                                             start=j == 0 and part == 0, stop=j == J - 1 and part == 2)
                    last.then_inc(a_mm, 1)

                def sum_up(g, k):
                    if not inside(g, k):
                        return
                    s = GS * g + k
                    pe.wait_ge(msg_l, s + 1)
                    if from_(g, k, 2):
                        pe.wait_ge(sum_added, s - 1)
                    for j in range(J):
                        for part in range(3):
                            last = te.matmul(psum[:, 4 + k % 2, 0:M], lhot[:, k, j, :], msgp[:, k % 2, part, j, :],
                                             start=j == 0 and part == 0, stop=j == J - 1 and part == 2)
                    last.then_inc(sum_mm, 1)

                def step(g, k):
                    turn(*shift(g, k, 1))
                    add_a(g, k)
                    sum_up(*shift(g, k, -1))
                in_groups(pe, step)

            @block.scalar
            def _(act):
                def step(g, k):
                    if inside(*shift(g, k, -1)):
                        s, q = GS * g + k - 1, (k - 1) % 2
                        act.wait_ge(msg_r, s + 1)
                        nc.scalar.copy(msgp[:, q, 1, :, :], msgr[:, q, :, :]).then_inc(msg_m, 1)
                    if inside(*shift(g, k, 1)):
                        gg, kk = shift(g, k, 1)
                        s, q = GS * g + k + 1, (k + 1) % 2
                        act.wait_ge(lo_hot_t, s + 1)
                        if from_(gg, kk, 2):
                            act.wait_ge(a_mm, s - 1)
                        nc.scalar.copy(lhot_t[:, q, :, :].rearrange("p j e -> p (j e)"), psumb[:, q, 0:T]).then_inc(lo_hot_out, 1)
                    if inside(g, k):
                        s, q = GS * g + k, k % 2
                        act.wait_ge(summed, s + 1)
                        if from_(g, k, 2):
                            act.wait_ge(sum_mm, s - 1)
                        nc.scalar.activation(msgp[:, q, 0, :, :], msg[:, q, :, :], ACT.Relu).then_inc(msg_h, 1)
                in_groups(act, step)

            @block.vector
            def _(dve):
                v = nc.vector
                dve.wait_ge(acc_clear, 1)

                def rows_of(g, k):
                    return rec2[:, ds(g % 2, 1), k, :, :].rearrange("p o j w -> p (o j) w")

                def one_hot(g, k):
                    if not inside(g, k):
                        return
                    s = GS * g + k
                    if k == 0:
                        arrived(g)
                    if from_(g, k, GS):
                        dve.wait_ge(sum_mm, s - GS + 1)
                    v.tensor_tensor(out=lhot[:, k, :, :], in0=iota[:, :].unsqueeze(1).broadcast_to([P, J, P]),
                                    in1=rows_of(g, k)[:, :, M:RW].broadcast_to([P, J, P]), op=ALU.is_equal).then_inc(lo_hot, 1)

                def arrived(g):
                    if isinstance(g, int):
                        dve.wait_ge(rows_in[g % 2], 16 * (g // 2 + 1))
                    else:
                        dve.wait_ge(rows_in[0], 16 * ((g + 2) // 2))
                        dve.wait_ge(rows_in[1], 16 * ((g + 1) // 2))

                def step(g, k):
                    before = shift(g, k, -1)
                    if inside(*before):
                        s, q = GS * g + k - 1, (k - 1) % 2
                        dve.wait_ge(msg_h, s + 1)
                        v.scalar_tensor_tensor(out=msgr[:, q, :, :].rearrange("p j m -> p (j m)"),
                                               in0=msg[:, q, :, :].rearrange("p j m -> p (j m)"), scalar=0.0,
                                               in1=msgp[:, q, 0, :, :].rearrange("p j m -> p (j m)"),
                                               op0=ALU.max, op1=ALU.subtract).then_inc(msg_r, 1)
                    one_hot(*shift(g, k, 2))
                    if inside(g, k):
                        s, q = GS * g + k, k % 2
                        dve.wait_ge(a_mm, s + 1)
                        if from_(g, k, 2):
                            dve.wait_ge(msg_r, s - 1)
                        v.tensor_tensor(out=msg[:, q, :, :], in0=psum[:, 2 + q, 0:J * M].rearrange("p (j m) -> p j m", j=J),
                                        in1=rows_of(g, k)[:, :, 0:M], op=ALU.add).then_inc(summed, 1)
                    if inside(*before):
                        s, q = GS * g + k - 1, (k - 1) % 2
                        dve.wait_ge(msg_m, s + 1)
                        v.tensor_tensor(out=msgp[:, q, 2, :, :], in0=msgr[:, q, :, :], in1=msgp[:, q, 1, :, :],
                                        op=ALU.subtract).then_inc(msg_l, 1)
                    if inside(*shift(g, k, -2)):
                        s, q = GS * g + k - 2, k % 2
                        bucket = dve.value_load(bucket_row[0:1, ds(s, 1)], min_val=0, max_val=SPARE)
                        dve.wait_ge(sum_mm, s + 1)
                        if from_(g, k, 3):
                            dve.wait_ge(sum_added, s)
                        a = acc[:, ds(bucket, 1), :].rearrange("p o m -> p (o m)")
                        v.tensor_tensor(out=a, in0=a, in1=psum[:, 4 + q, 0:M], op=ALU.add).then_inc(sum_added, 1)
                in_groups(dve, step)

        x_again, sums_t, sums_out, y_mm = sem("x_again"), sem("sums_t"), sem("sums_out"), sem("y_mm")
        z_ready, y_ready, y_out, x_free = sem("z_ready"), sem("y_ready"), sem("y_out"), sem("x_free")
        with ExitStack() as tmp:
            xf = sb("xf", [P, NG, FG, F], f32, tmp)
            st = sb("st", [P, 2, P], f32, tmp)
            z = sb("z", [P, 2, FG * F], f32, tmp)
            LB = NB - (NG - 1) * FG
            x_clear = sem("x_clear")
            cp = sb("cp", [P, 2, P], f32, tmp)
            sums_cp = sem("sums_cp")
            assert NG % 2 == 1

            def finish(eng, step):
                for k in range(2):
                    step(k, k, FG)
                with eng.Fori(1, NG // 2) as i:
                    for k in range(2):
                        step(2 * i + k, k, FG)
                step(NG - 1, 0, LB)

            block = tmp.enter_context(nc.Block())

            @block.sync
            def _(sp):
                main = (NB - 1) * P
                xb_ = xf[:, :, :, :].rearrange("p g q f -> p (g q) f")
                sp.dma_start(xb_[:, 0:NB - 1, :], x[0:main, :].rearrange("(b p) f -> p b f", p=P)).then_inc(x_again, 16)
                sp.wait_ge(x_clear, 1)
                sp.dma_start(xb_[0:NTAIL, NB - 1, :], x[main:N, :]).then_inc(x_again, 16)
                with sp.Fori(0, NG - 1) as g:
                    sp.wait_ge(y_ready, g + 1)
                    sp.dma_start(y[ds(g * (FG * P), FG * P), :].rearrange("(q p) f -> p q f", p=P),
                                 xf[:, ds(g, 1), :, :].rearrange("p o q f -> p (o q) f")).then_inc(y_out, 16)
                sp.wait_ge(y_ready, NG)
                r0 = (NG - 1) * FG * P
                sp.dma_start(y[r0:main, :].rearrange("(q p) f -> p q f", p=P), xf[:, NG - 1, 0:LB - 1, :]).then_inc(y_out, 16)
                sp.dma_start(y[main:N, :], xf[0:NTAIL, NG - 1, LB - 1, :]).then_inc(y_out, 16)
                sp.wait_ge(y_out, 16 * (NG + 1))

            @block.gpsimd
            def _(pool):
                pool.memset(xf[:, NG - 1, LB - 1, :], 0.0).then_inc(x_clear, 1)

            @block.tensor
            def _(pe):
                def step(g, k, nb):
                    later = not (isinstance(g, int) and g < 2)
                    pe.wait_ge(sums_cp, g + 1)
                    if later:
                        pe.wait_ge(sums_out, g - 1)
                    nc.tensor.transpose(psum[:, k, 0:P], cp[:, k, :], identf[:, :]).then_inc(sums_t, 1)
                    pe.wait_ge(sums_out, g + 1)
                    if later:
                        pe.wait_ge(z_ready, g - 1)
                    nc.tensor.matmul(psum[:, 2 + k, 0:nb * F], st[:, k, :],
                                     w_sum[:, 0:nb, :].rearrange("p q f -> p (q f)"), start=True, stop=True).then_inc(y_mm, 1)
                finish(pe, step)

            @block.scalar
            def _(act):
                def copy(g, k):
                    later = not (isinstance(g, int) and g < 2)
                    if later:
                        act.wait_ge(sums_t, g - 1)
                    nc.scalar.copy(cp[:, k, :], acc[:, ds(g * FG, FG), :].rearrange("p q m -> p (q m)")).then_inc(sums_cp, 1)

                def step(g, k, nb):
                    later = not (isinstance(g, int) and g < 2)
                    copy(g, k)
                    act.wait_ge(sums_t, g + 1)
                    if later:
                        act.wait_ge(y_mm, g - 1)
                    nc.scalar.copy(st[:, k, :], psum[:, k, 0:P]).then_inc(sums_out, 1)
                finish(act, step)

            @block.vector
            def _(dve):
                v = nc.vector
                dve.wait_ge(x_again, 32)

                def step(g, k, nb):
                    later = not (isinstance(g, int) and g < 2)
                    dve.wait_ge(y_mm, g + 1)
                    if later:
                        dve.wait_ge(y_ready, g - 1)
                    v.tensor_tensor(out=z[:, k, 0:nb * F], in0=psum[:, 2 + k, 0:nb * F],
                                    in1=ypart[:, ds(g * FG, nb), :].rearrange("p q f -> p (q f)"), op=ALU.add).then_inc(z_ready, 1)
                    dve.wait_ge(z_ready, g + 1)
                    xg = xf[:, ds(g, 1), 0:nb, :].rearrange("p o q f -> p (o q f)")
                    v.scalar_tensor_tensor(out=xg, in0=z[:, k, 0:nb * F], scalar=0.0, in1=xg, op0=ALU.max, op1=ALU.add)\
                        .then_inc(y_ready, 1)
                finish(dve, step)


def kernel(x, src, dst, edge_attr_64, L0_gnn_W_edge, L0_gnn_b_edge, L0_gnn_W_node, L0_gnn_b_node):
    import numpy as np
    import concourse.bacc as bacc
    from concourse import mybir as mb
    from concourse.bass_utils import run_bass_kernel_spmd

    ins = {"x": x, "src": src, "dst": dst, "edge_attr": edge_attr_64, "w_edge": L0_gnn_W_edge,
           "b_edge": L0_gnn_b_edge, "w_node": L0_gnn_W_node, "b_node": L0_gnn_b_node}
    nc = bacc.Bacc("TRN2", target_bir_lowering=False, num_devices=1)
    arrays, aps = {}, []
    for name, a in ins.items():
        a = np.ascontiguousarray(a)
        arrays[name] = a
        aps.append(nc.dram_tensor(name, a.shape, mb.dt.from_np(a.dtype), kind="ExternalInput").ap())
    out = nc.dram_tensor("y", tuple(x.shape), mb.dt.float32, kind="ExternalOutput").ap()
    gnn_layer(nc, *aps, out)
    r = run_bass_kernel_spmd(nc, [arrays], core_ids=[0])
    return r.results[0]["y"]
```

```python
import concourse.bass as bass
from concourse import mybir
from contextlib import ExitStack


def gnn_layer(nc, x, src, dst, ef, w_edge, b_edge, w_node, b_node, y):
    f32, bf16, i32 = mybir.dt.float32, mybir.dt.bfloat16, mybir.dt.int32
    ALU = mybir.AluOpType
    ACT = mybir.ActivationFunctionType
    AX = mybir.AxisListType.X
    ds = bass.ds

    P = 128
    N, F = x.shape
    E, FE = ef.shape
    M = w_edge.shape[1]
    J = 4
    T = P * J
    NS = -(-E // T)
    LAST0 = E - T
    SEEN = (NS * T - E) // J
    assert (NS * T - E) % J == 0 and NS % 2 == 0
    SB = -(-NS // P)
    NB = -(-N // P)
    NTAIL = N - (NB - 1) * P
    NS2 = -(-(E // T + NB + 1) // 12) * 12
    assert NS2 * T >= E + NB * (T - 1)
    ROWS = NS2 * T
    RW = M + 1
    SPARE = NB
    CB = 14
    NC = NB // CB
    assert NC * CB == NB
    WC = F + 2 * M
    FG = 4
    NG = -(-NB // FG)

    rows = nc.dram_tensor("edge_rows", (ROWS, RW), f32, kind="Internal").ap()
    b_parts = nc.dram_tensor("b_parts", ((NB + 1) * P, 3 * M), bf16, kind="Internal").ap()
    b_rows = nc.dram_tensor("b_rows", (NB * P, M), f32, kind="Internal").ap()
    bucket_dram = nc.dram_tensor("bucket_of", (1, P * 8), i32, kind="Internal").ap()

    ctx = ExitStack()
    with ctx:
        def sb(name, shape, dt, where=ctx):
            return where.enter_context(nc.sbuf_tensor(name, shape, dt))

        def sem(name):
            return ctx.enter_context(nc.semaphore(name))

        psum = ctx.enter_context(nc.psum_tensor("psum", [P, 8, 512], f32))
        psumb = psum[:, :, :].bitcast(bf16)

        ident = sb("ident", [P, P], bf16)
        identf = sb("identf", [P, P], f32)
        ones = sb("ones", [P, P], bf16)
        onesf = sb("onesf", [P, P], f32)
        upper = sb("upper", [P, P], bf16)
        iota_i = sb("iota_i", [P, P], i32)
        part_i = sb("part_i", [P, 1], i32)
        sidx_i = sb("sidx_i", [P, 8], i32)
        iota = sb("iota", [P, P], bf16)
        iotaf = sb("iotaf", [P, P], f32)
        partf = sb("partf", [P, 1], f32)
        sidx = sb("sidx", [P, 8], f32)
        eps = sb("eps", [P, 1], f32)
        FILL = ROWS * RW // P // 96
        filler = sb("filler", [P, FILL], f32)
        assert 96 * P * FILL == ROWS * RW
        wcat = sb("wcat", [P, WC], f32)
        bias = sb("bias", [P, WC], f32)
        w_ef = sb("w_ef", [P, 2 * M], f32)
        w_sum = sb("w_sum", [P, FG, F], f32)
        hi_col = sb("hi_col", [P, SB * P, J], bf16)
        lo_col = sb("lo_col", [P, SB * P, J], bf16)
        dst_col = sb("dst_col", [P, SB * P, J], i32)
        rel_row = sb("rel_row", [P, SB, T], bf16)
        base = sb("base", [P, NB], f32)
        match = sb("match", [P, 1], f32)
        general_i = sb("general_i", [P, 1], i32)
        bucket_row = sb("bucket_row", [1, P * 8], i32)
        a_tab = sb("a_tab", [P, NB + 1, 3, M], bf16)
        ypart = sb("ypart", [P, NB, F], f32)

        consts, cast = sem("consts"), sem("cast")
        weights_in, idx_in, idx_clear = sem("weights_in"), sem("idx_in"), sem("idx_clear")
        w_clear = sem("w_clear")
        filled = sem("filled")
        dve_e, cols_t, cols_out = sem("dve_e"), sem("cols_t"), sem("cols_out")
        idx_rows, viol_ready, counted, buckets_ready = sem("idx_rows"), sem("viol_ready"), sem("counted"), sem("buckets_ready")
        dcols_out, count_mm, flag_mm = sem("dcols_out"), sem("count_mm"), sem("flag_mm")
        bucket_out, bucket_in = sem("bucket_out"), sem("bucket_in")
        with ExitStack() as tmp:
            src_row = sb("src_row", [P, SB, T], i32, tmp)
            dst_row = sb("dst_row", [P, SB, T], i32, tmp)
            t1 = sb("t1", [P, SB, T], i32, tmp)
            t2 = sb("t2", [P, SB, T], i32, tmp)
            hi_row = sb("hi_row", [P, SB, T], bf16, tmp)
            lo_row = sb("lo_row", [P, SB, T], bf16, tmp)
            spans = sb("spans", [P, 4, SB], f32, tmp)
            viol = sb("viol", [P, 1], f32, tmp)
            violb = sb("violb", [P, 1], bf16, tmp)
            part_counts = sb("part_counts", [P, NB], f32, tmp)
            c_f = sb("c_f", [P, 3, NB], f32, tmp)
            c_i = sb("c_i", [P, 2, NB], i32, tmp)
            cmp = sb("cmp", [P, 8, NB], f32, tmp)
            bk_f = sb("bk_f", [P, 8], f32, tmp)
            bk_i = sb("bk_i", [P, 8], i32, tmp)
            REST = NS - 1 - (SB - 1) * P
            block = tmp.enter_context(nc.Block())

            @block.sync
            def _(sp):
                full = (SB - 1) * P * T
                for row, arr in ((src_row, src), (dst_row, dst)):
                    sp.dma_start(row[:, 0:SB - 1, :], arr[0:full].rearrange("(b s e) -> s b e", s=P, e=T)).then_inc(idx_in, 16)
                sp.wait_ge(idx_clear, 2)
                for row, arr in ((src_row, src), (dst_row, dst)):
                    sp.dma_start(row[0:REST, SB - 1, :], arr[full:full + REST * T].rearrange("(s e) -> s e", e=T)).then_inc(idx_in, 16)
                    sp.dma_start(row[REST:REST + 1, SB - 1, :], arr[LAST0:E].rearrange("(s e) -> s e", e=T)).then_inc(idx_in, 16)
                sp.wait_ge(buckets_ready, 1)
                sp.dma_start(bucket_dram.rearrange("o (p c) -> (o p) c", c=8), bk_i[:, :]).then_inc(bucket_out, 16)
                sp.wait_ge(bucket_out, 16)
                sp.dma_start(bucket_row[:, :], bucket_dram).then_inc(bucket_in, 16)
                sp.wait_ge(bucket_in, 16)

            @block.gpsimd
            def _(pool):
                pool.memset(src_row[:, SB - 1, :], 0).then_inc(idx_clear, 1)
                pool.memset(dst_row[:, SB - 1, :], 0).then_inc(idx_clear, 1)
                pool.memset(filler[:, :], -1.0).then_inc(consts, 1)
                pool.memset(w_ef[:, :], 0.0).then_inc(w_clear, 1)
                pool.memset(w_sum[:, :, :], 0.0).then_inc(w_clear, 1)
                pool.memset(bias[:, F:F + M], 0.0).then_inc(w_clear, 1)
                pool.memset(ones[:, :], 1.0).then_inc(consts, 1)
                pool.memset(onesf[:, :], 1.0).then_inc(consts, 1)
                pool.memset(eps[:, :], 1e-5).then_inc(consts, 1)
                pool.memset(ident[:, :], 0.0).then_inc(consts, 1)
                pool.memset(identf[:, :], 0.0).then_inc(consts, 1)
                pool.iota(iota_i[:, :], pattern=[[1, P]], base=0, channel_multiplier=0).then_inc(consts, 1)
                pool.iota(part_i[:, :], pattern=[[0, 1]], base=0, channel_multiplier=1).then_inc(consts, 1)
                pool.iota(sidx_i[:, :], pattern=[[1, 8]], base=0, channel_multiplier=8).then_inc(consts, 1)
                pool.wait_ge(consts, 9)
                for m in (ident, identf):
                    pool.affine_select(out=m[:, :], in_=m[:, :], compare_op=ALU.not_equal, fill=1.0, base=0,
                                       pattern=[[-1, P]], channel_multiplier=1).then_inc(consts, 1)
                pool.affine_select(out=upper[:, :], in_=ones[:, :], compare_op=ALU.is_gt, fill=0.0, base=0,
                                   pattern=[[1, P]], channel_multiplier=-1).then_inc(consts, 1)

            @block.vector
            def _(dve):
                n = [0]

                def link(ins, signal=None):
                    if signal is not None:
                        ins.then_inc(signal, 1)
                        dve.wait_ge(signal, 1)
                        return
                    n[0] += 1
                    ins.then_inc(dve_e, 1)
                    dve.wait_ge(dve_e, n[0])

                v = nc.vector
                dve.wait_ge(consts, 12)
                v.tensor_copy(iota[:, :], iota_i[:, :]).then_inc(cast, 1)
                v.tensor_copy(iotaf[:, :], iota_i[:, :]).then_inc(cast, 1)
                v.tensor_copy(partf[:, :], part_i[:, :]).then_inc(cast, 1)
                v.tensor_copy(sidx[:, :], sidx_i[:, :]).then_inc(cast, 1)
                dve.wait_ge(idx_in, 16 * 6)
                link(v.tensor_single_scalar(t1[:, :, :], src_row[:, :, :], P.bit_length() - 1, ALU.arith_shift_right))
                link(v.tensor_single_scalar(t2[:, :, :], src_row[:, :, :], P - 1, ALU.bitwise_and))
                link(v.tensor_copy(hi_row[:, :, :], t1[:, :, :]))
                link(v.tensor_copy(lo_row[:, :, :], t2[:, :, :]))
                dst_f, rel = t1[:, :, :].bitcast(f32), t2[:, :, :].bitcast(f32)
                link(v.tensor_copy(dst_f, dst_row[:, :, :]), idx_rows)
                link(v.tensor_tensor(out=rel, in0=dst_f, in1=dst_f[:, :, 0:1].broadcast_to([P, SB, T]), op=ALU.subtract))
                for b in range(SB):
                    link(v.tensor_copy(rel_row[:, b, :].rearrange("s (j p) -> s p j", j=J),
                                       rel[:, b, :].rearrange("s (p j) -> s p j", j=J)))
                link(v.tensor_reduce(out=spans[:, 0, :], in_=rel, op=ALU.max, axis=AX))
                link(v.tensor_reduce(out=spans[:, 1, :], in_=rel, op=ALU.min, axis=AX))
                link(v.tensor_single_scalar(spans[:, 2, :], spans[:, 0, :], float(P), ALU.is_ge))
                link(v.tensor_single_scalar(spans[:, 3, :], spans[:, 1, :], 0.0, ALU.is_lt))
                link(v.tensor_reduce(out=viol[:, :], in_=spans[:, 2:4, :].rearrange("p a b -> p (a b)"), op=ALU.add, axis=AX))
                link(v.tensor_copy(violb[:, :], viol[:, :]), viol_ready)
                for b in range(SB):
                    dve.wait_ge(cols_t, b + 1)
                    v.tensor_copy(dst_col[:, b * P:(b + 1) * P, :],
                                  psum[:, 4 + b % 2, :].rearrange("p (j s) -> p s j", j=J)).then_inc(dcols_out, 1)
                dve.wait_ge(flag_mm, 1)
                link(v.tensor_scalar(viol[:, :], psum[:, 6, 0:1], 1.0, None, ALU.min))
                link(v.tensor_copy(general_i[:, :], viol[:, :]))
                link(v.scalar_tensor_tensor(out=match[:, :], in0=viol[:, :], scalar=0.5, in1=partf[:, :], op0=ALU.mult, op1=ALU.add))
                dve.wait_ge(cols_out, 2 * SB)
                link(v.memset(hi_col[0:SEEN, NS - 1, :], float(P - 1)))
                flat = hi_col[:, 0:NS, :].rearrange("p s j -> p (s j)")
                junk = hi_row[:, :, :].rearrange("p b e -> p (b e)")[:, 0:NS * J]
                with dve.Fori(0, NB) as h:
                    v.tensor_scalar(junk, flat, iotaf[:, ds(h, 1)], 0.0, ALU.is_equal, ALU.add,
                                    accum_out=part_counts[:, ds(h, 1)]).then_inc(counted, 1)
                    dve.wait_ge(counted, h + 1)
                dve.wait_ge(count_mm, 1)
                link(v.tensor_scalar(c_f[:, 0, :], psum[:, 7, 0:NB], float(T - 1), None, ALU.add))
                link(v.tensor_copy(c_i[:, 0, :], c_f[:, 0, :]))
                link(v.tensor_single_scalar(c_i[:, 1, :], c_i[:, 0, :], T.bit_length() - 1, ALU.arith_shift_right))
                link(v.tensor_copy(c_f[:, 0, :], c_i[:, 1, :]))
                link(v.tensor_tensor_scan(out=c_f[:, 1, :], data0=onesf[:, 0:NB], data1=c_f[:, 0, :], initial=0.0,
                                          op0=ALU.mult, op1=ALU.add))
                link(v.tensor_tensor(out=cmp[:, :, :], in0=c_f[:, 1:2, :].broadcast_to([P, 8, NB]),
                                     in1=sidx[:, :].unsqueeze(2).broadcast_to([P, 8, NB]), op=ALU.is_le))
                link(v.tensor_tensor(out=c_f[:, 2, :], in0=c_f[:, 1, :], in1=c_f[:, 0, :], op=ALU.subtract))
                link(v.tensor_scalar(base[:, :], c_f[:, 2, :], float(T), None, ALU.mult))
                link(v.tensor_reduce(out=bk_f[:, :], in_=cmp[:, :, :], op=ALU.add, axis=AX))
                link(v.tensor_copy(bk_i[:, :], bk_f[:, :]), buckets_ready)

            @block.tensor
            def _(pe):
                pe.wait_ge(consts, 12)
                pe.wait_ge(idx_rows, 1)
                for b in range(SB):
                    if b >= 2:
                        pe.wait_ge(cols_out, 2 * (b - 1))
                        pe.wait_ge(dcols_out, b - 1)
                    for bank, row, idn in ((0, hi_row, ident), (2, lo_row, ident), (4, t1[:, :, :].bitcast(f32), identf)):
                        for j in range(J):
                            out = psum[:, 4 + b % 2, j * P:(j + 1) * P] if bank == 4 else psumb[:, bank + b % 2, j * P:(j + 1) * P]
                            last = nc.tensor.transpose(out, row[:, b, :].rearrange("s (p j) -> s j p", j=J)[:, j, :], idn[:, :])
                    last.then_inc(cols_t, 1)
                pe.wait_ge(viol_ready, 1)
                nc.tensor.matmul(psum[:, 6, 0:1], ones[:, :], violb[:, :], start=True, stop=True).then_inc(flag_mm, 1)
                pe.wait_ge(counted, NB)
                nc.tensor.matmul(psum[:, 7, 0:NB], onesf[:, :], part_counts[:, :], start=True, stop=True).then_inc(count_mm, 1)

            @block.scalar
            def _(act):
                act.wait_ge(w_clear, 3)
                act.dma_start(wcat[:, 0:F], w_node[0:F, :]).then_inc(weights_in, 16)
                act.dma_start(wcat[:, F:F + M], w_edge[0:F, :]).then_inc(weights_in, 16)
                act.dma_start(wcat[:, F + M:WC], w_edge[F:2 * F, :]).then_inc(weights_in, 16)
                for q in range(2):
                    act.dma_start(w_ef[q * FE:(q + 1) * FE, q * M:(q + 1) * M], w_edge[2 * F:2 * F + FE, :]).then_inc(weights_in, 16)
                for q in range(FG):
                    act.dma_start(w_sum[q * M:(q + 1) * M, q, :], w_node[F:F + M, :]).then_inc(weights_in, 16)
                act.dma_start(bias[:, 0:F], b_node.unsqueeze(0).broadcast_to([P, F])).then_inc(weights_in, 16)
                act.dma_start(bias[:, F + M:WC], b_edge.unsqueeze(0).broadcast_to([P, M])).then_inc(weights_in, 16)
                act.wait_ge(consts, 1)
                reps = ROWS * RW // (P * FILL)
                act.dma_start(rows.rearrange("r c -> (r c)").rearrange("(p a c) -> p a c", p=P, c=FILL),
                              filler[:, :].unsqueeze(1).broadcast_to([P, reps, FILL])).then_inc(filled, 16)
                for b in range(SB):
                    act.wait_ge(cols_t, b + 1)
                    for bank, col in ((0, hi_col), (2, lo_col)):
                        nc.scalar.copy(col[:, b * P:(b + 1) * P, :],
                                       psumb[:, bank + b % 2, 0:T].rearrange("p (j s) -> p s j", j=J)).then_inc(cols_out, 1)

        x_in = [sem("x_in0"), sem("x_in1")]
        row_sum, mean, centred, sq_done = sem("row_sum"), sem("mean"), sem("centred"), sem("sq_done")
        sq_sum, std_done, inv_std = sem("sq_sum"), sem("std_done"), sem("inv_std")
        h_ready, ht_t, ht_out = sem("h_ready"), sem("ht_t"), sem("ht_out")
        node_mm, node_out = sem("node_mm"), sem("node_out")
        part_h, part_r, part_m, part_l = sem("part_h"), sem("part_r"), sem("part_m"), sem("part_l")
        b_out, spare_clear, spare_out, tabs_done = sem("b_out"), sem("spare_clear"), sem("spare_out"), sem("tabs_done")
        with ExitStack() as tmp:
            xb = sb("xb", [P, 2, CB, F], f32, tmp)
            xc = sb("xc", [P, CB, F], f32, tmp)
            sq = sb("sq", [P, CB, F], f32, tmp)
            hn = sb("hn", [P, CB, F], f32, tmp)
            ht = sb("ht", [P, 2, P], f32, tmp)
            stat = sb("stat", [P, 5, CB], f32, tmp)
            ab = sb("ab", [P, CB, 2 * M], f32, tmp)
            rest = sb("rest", [P, CB, 2 * M], f32, tmp)
            abp = sb("abp", [P, 3, CB, 2 * M], bf16, tmp)
            bst = sb("bst", [P, CB, 3, M], bf16, tmp)
            block = tmp.enter_context(nc.Block())

            @block.sync
            def _(sp):
                def load(c, k, whole):
                    r0 = c * (CB * P)
                    sp.dma_start(xb[:, k, 0:CB - 1, :],
                                 x[ds(r0, (CB - 1) * P), :].rearrange("(b p) f -> p b f", p=P)).then_inc(x_in[k], 16)
                    n = P if whole else NTAIL
                    sp.dma_start(xb[0:n, k, CB - 1, :], x[ds(r0 + (CB - 1) * P, n), :]).then_inc(x_in[k], 16)

                def store(c):
                    sp.wait_ge(tabs_done, 4 * (c + 1))
                    sp.dma_start(b_parts[ds(c * (CB * P), CB * P), :].rearrange("(b p) m -> p b m", p=P),
                                 bst[:, :, :, :].rearrange("p b t m -> p b (t m)")).then_inc(b_out, 16)
                    sp.dma_start(b_rows[ds(c * (CB * P), CB * P), :].rearrange("(b p) m -> p b m", p=P),
                                 ab[:, :, M:2 * M]).then_inc(b_out, 16)

                for c in range(NC):
                    if c >= 2:
                        sp.wait_ge(centred, c - 1)
                    load(c, c % 2, c < NC - 1)
                    if c >= 1:
                        store(c - 1)
                store(NC - 1)
                sp.wait_ge(b_out, 32 * NC)

            @block.gpsimd
            def _(pool):
                pool.memset(a_tab[:, NB, :, :], 0.0).then_inc(spare_clear, 1)
                pool.memset(bst[:, 0, :, :], 0.0).then_inc(spare_clear, 1)
                pool.wait_ge(spare_clear, 2)
                pool.dma_start(b_parts[NB * P:(NB + 1) * P, :], bst[:, 0, :, :].rearrange("p t m -> p (t m)")).then_inc(spare_out, 16)
                pool.wait_ge(spare_out, 16)

            @block.vector
            def _(dve):
                v = nc.vector
                dve.wait_ge(spare_out, 16)
                with dve.Fori(0, NC) as c:
                    xs = xb[:, ds(c % 2, 1), :, :].rearrange("p o b f -> p (o b) f")

                    def done(ins, signal):
                        ins.then_inc(signal, 1)
                        dve.wait_ge(signal, c + 1)

                    def bc(i):
                        return stat[:, i, :].unsqueeze(2).broadcast_to([P, CB, F])

                    dve.wait_ge(x_in[0], 32 * ((c + 2) // 2))
                    dve.wait_ge(x_in[1], 32 * ((c + 1) // 2))
                    done(v.tensor_reduce(out=stat[:, 0, :], in_=xs, op=ALU.add, axis=AX), row_sum)
                    done(v.tensor_scalar(stat[:, 1, :], stat[:, 0, :], 1.0 / F, None, ALU.mult), mean)
                    done(v.tensor_tensor(out=xc[:, :, :], in0=xs, in1=bc(1), op=ALU.subtract), centred)
                    dve.wait_ge(sq_done, c + 1)
                    done(v.tensor_reduce(out=stat[:, 2, :], in_=sq[:, :, :], op=ALU.add, axis=AX), sq_sum)
                    dve.wait_ge(std_done, c + 1)
                    done(v.reciprocal(stat[:, 4, :], stat[:, 3, :]), inv_std)
                    done(v.tensor_tensor(out=hn[:, :, :], in0=xc[:, :, :], in1=bc(4), op=ALU.mult), h_ready)
                    for b in range(CB):
                        dve.wait_ge(node_mm, c * CB + (b + 1))
                        bank = 2 + b % 2
                        v.tensor_tensor(out=ypart[:, ds(c * CB + b, 1), :].rearrange("p o f -> p (o f)"),
                                        in0=psum[:, bank, 0:F], in1=bias[:, 0:F], op=ALU.add)
                        if b == 0:
                            dve.wait_ge(b_out, 32 * c)
                        v.tensor_tensor(out=ab[:, b, :], in0=psum[:, bank, F:WC], in1=bias[:, F:WC], op=ALU.add)\
                            .then_inc(node_out, 1)
                    dve.wait_ge(part_h, c + 1)
                    done(v.tensor_tensor(out=rest[:, :, :], in0=ab[:, :, :], in1=abp[:, 0, :, :], op=ALU.subtract), part_r)
                    dve.wait_ge(part_m, c + 1)
                    done(v.tensor_tensor(out=abp[:, 2, :, :], in0=rest[:, :, :], in1=abp[:, 1, :, :], op=ALU.subtract), part_l)
                    for t in range(3):
                        v.tensor_copy(bst[:, :, t, :], abp[:, t, :, M:2 * M])
                        last = v.tensor_copy(a_tab[:, ds(c * CB, CB), t, :], abp[:, t, :, 0:M])
                    last.then_inc(tabs_done, 4)
                    dve.wait_ge(tabs_done, 4 * (c + 1))

            @block.tensor
            def _(pe):
                pe.wait_ge(weights_in, 16 * (5 + FG + 2))
                with pe.Fori(0, NC) as c:
                    pe.wait_ge(h_ready, c + 1)

                    def transpose(b):
                        if b >= 2:
                            pe.wait_ge(ht_out, c * CB + (b - 1))
                        nc.tensor.transpose(psum[:, b % 2, 0:P], hn[:, b, :], identf[:, :]).then_inc(ht_t, 1)

                    transpose(0)
                    for b in range(CB):
                        if b + 1 < CB:
                            transpose(b + 1)
                        pe.wait_ge(ht_out, c * CB + (b + 1))
                        if b >= 2:
                            pe.wait_ge(node_out, c * CB + (b - 1))
                        nc.tensor.matmul(psum[:, 2 + b % 2, 0:WC], ht[:, b % 2, :], wcat[:, :], start=True, stop=True)\
                            .then_inc(node_mm, 1)
                    pe.wait_ge(node_out, (c + 1) * CB)

            @block.scalar
            def _(act):
                a = nc.scalar
                with act.Fori(0, NC) as c:
                    act.wait_ge(centred, c + 1)
                    a.activation(sq[:, :, :], xc[:, :, :], ACT.Square).then_inc(sq_done, 1)
                    act.wait_ge(sq_sum, c + 1)
                    a.activation(stat[:, 3, :], stat[:, 2, :], ACT.Sqrt, bias=eps[:, :], scale=1.0 / F).then_inc(std_done, 1)
                    for b in range(CB):
                        act.wait_ge(ht_t, c * CB + (b + 1))
                        if b >= 2:
                            act.wait_ge(node_mm, c * CB + (b - 1))
                        a.activation(ht[:, b % 2, :], psum[:, b % 2, 0:P], ACT.Relu).then_inc(ht_out, 1)
                    act.wait_ge(node_out, (c + 1) * CB)
                    a.copy(abp[:, 0, :, :], ab[:, :, :]).then_inc(part_h, 1)
                    act.wait_ge(part_r, c + 1)
                    a.copy(abp[:, 1, :, :], rest[:, :, :]).then_inc(part_m, 1)

        ef_in = [sem("ef_in0"), sem("ef_in1")]
        bw_in = [sem("bw_in0"), sem("bw_in1")]
        scattered = [sem("scattered0"), sem("scattered1")]
        gathered_dma, gathered, gidx_ready = sem("gathered_dma"), sem("gathered"), sem("gidx_ready")
        g_clear, pool_turns = sem("g_clear"), sem("pool_turns")
        ef_t, ef_out, rel_bc = sem("ef_t"), sem("ef_out"), sem("rel_bc")
        window, onehot, ranks, pre = sem("window"), sem("onehot"), sem("ranks"), sem("pre")
        dve_p, pos_ready, rec_ready, lo_ready = sem("dve_p"), sem("pos_ready"), sem("rec_ready"), sem("lo_ready")
        ranks_read, tail_pos = sem("ranks_read"), sem("tail_pos")
        with ExitStack() as tmp:
            eft_in = sb("eft_in", [P, 2, J, FE], f32, tmp)
            eft = sb("eft", [P, 2, 2 * P], f32, tmp)
            bwin = sb("bwin", [P, 2, 3, M], bf16, tmp)
            win = sb("win", [P, 2, T], bf16, tmp)
            hot = sb("hot", [P, 2, J, NB], bf16, tmp)
            s1 = sb("s1", [P, J, NB], f32, tmp)
            s2 = sb("s2", [P, J, NB], f32, tmp)
            pos_f = sb("pos_f", [P, J], f32, tmp)
            pos = sb("pos", [P, 2, J], i32, tmp)
            rec = sb("rec", [P, 2, J, RW], f32, tmp)
            gat = sb("gat", [P, 2, J, M], f32, tmp)
            gidx = sb("gidx", [P, 2, J], i32, tmp)
            block = tmp.enter_context(nc.Block())

            def in_pairs(eng, step):
                for k in range(2):
                    step(0, k)
                with eng.Fori(1, NS // 2 - 1) as i:
                    for k in range(2):
                        step(i, k)
                for k in range(2):
                    step(NS // 2 - 1, k)

            def after(i, k, n=1):
                return i + (k + n) // 2, (k + n) % 2

            def start_of(i, k):
                return LAST0 if isinstance(i, int) and 2 * i + k == NS - 1 else (2 * i + k) * T

            def exists(i, k):
                return not isinstance(i, int) or 0 <= 2 * i + k < NS

            @block.sync
            def _(sp):
                def step(i, k):
                    t, e0 = 2 * i + k, start_of(i, k)
                    later = not (isinstance(i, int) and i == 0)
                    if later:
                        sp.wait_ge(ef_t, t - 1)
                    sp.dma_start(eft_in[:, k, :, :].rearrange("p j f -> p (j f)"),
                                 ef[ds(e0, T), :].rearrange("(p j) f -> p (j f)", j=J)).then_inc(ef_in[k], 16)
                    first = sp.value_load(dst[ds(e0, 1)].rearrange("(a b) -> a b", a=1), min_val=0, max_val=N - 1)
                    if later:
                        sp.wait_ge(pre, t - 1)
                    sp.dma_start(bwin[:, k, :, :].rearrange("p t m -> p (t m)"), b_parts[ds(first, P), :]).then_inc(bw_in[k], 16)
                in_pairs(sp, step)

            @block.gpsimd
            def _(pool):
                pool.memset(gat[:, :, :, :], 0.0).then_inc(g_clear, 1)
                pool.wait_ge(g_clear, 1)
                pool.wait_ge(filled, 16)

                def step(i, k, general):
                    t = 2 * i + k
                    later = not (isinstance(i, int) and i == 0)
                    if general:
                        if later:
                            pool.wait_ge(rec_ready, t - 1)
                        pool.tensor_copy(gidx[:, k, :], dst_col[:, ds(t, 1), :].rearrange("p o j -> p (o j)")).then_inc(gidx_ready, 1)
                        pool.wait_ge(gidx_ready, t + 1)
                        pool.sem_inc(pool_turns, 1)
                        for j in range(J):
                            pool.indirect_dma_start(out=gat[:, k, j, :], out_offset=None, in_=b_rows[:, :],
                                                    in_offset=bass.IndirectOffsetOnAxis(ap=gidx[:, k, j:j + 1], axis=0))\
                                .then_inc(gathered_dma, 16)
                        pool.wait_ge(gathered_dma, 16 * J * (t + 1))
                        pool.sem_inc(gathered, 1)
                    pool.wait_ge(pos_ready, t + 1)
                    pool.wait_ge(lo_ready, t + 1)
                    pool.wait_ge(rec_ready, t + 1)
                    pool.sem_inc(pool_turns, 1)
                    for j in range(J):
                        pool.indirect_dma_start(out=rows[:, :], out_offset=bass.IndirectOffsetOnAxis(ap=pos[:, k, j:j + 1], axis=0),
                                                in_=rec[:, k, j, :], in_offset=None,
                                                bounds_check=ROWS - 1, oob_is_err=False).then_inc(scattered[k], 16)

                flag = pool.value_load(general_i[0:1, 0:1], min_val=0, max_val=1)
                with pool.If(flag != 0):
                    in_pairs(pool, lambda i, k: step(i, k, True))
                with pool.Else():
                    pool.sem_inc(gathered, NS)
                    in_pairs(pool, lambda i, k: step(i, k, False))
                for k in range(2):
                    pool.wait_ge(scattered[k], 16 * J * (NS // 2))

            @block.tensor
            def _(pe):
                te = nc.tensor

                def spread(i, k):
                    if not exists(i, k):
                        return
                    t = 2 * i + k
                    later = not (isinstance(i, int) and i == 0)
                    if later:
                        pe.wait_ge(ef_out, t - 1)
                    pe.wait_ge(ef_in[k], 16 * (i + 1))
                    for q in range(2):
                        last = te.transpose(psum[:, k, q * P:(q + 1) * P],
                                            eft_in[:, k, 2 * q:2 * q + 2, :].rearrange("p j f -> p (j f)"), identf[:, :])
                    last.then_inc(ef_t, 1)
                    if later:
                        pe.wait_ge(window, t - 1)
                    te.matmul(psum[:, 2 + k, :], ident[:, ds(t % P, 1)].broadcast_to([P, P]),
                              rel_row[:, ds(t // P, 1), :].rearrange("s o e -> s (o e)"), start=True, stop=True).then_inc(rel_bc, 1)

                def step(i, k):
                    t = 2 * i + k
                    later = not (isinstance(i, int) and i == 0)
                    spread(*after(i, k))
                    cum = psum[:, 4 + k, :]
                    h = hot[:, k, :, :].rearrange("p j b -> p (j b)")
                    pe.wait_ge(onehot, t + 1)
                    if later:
                        pe.wait_ge(ranks_read, t - 1)
                    te.matmul(cum[:, 0:J * NB], upper[:, :], h, start=True, stop=False)
                    te.matmul(cum[:, J * NB:(J + 1) * NB], ones[:, :], h[:, (J - 1) * NB:], start=False, stop=False)
                    te.matmul(cum[:, NB:J * NB], ones[:, :], h[:, 0:(J - 1) * NB], start=False, stop=False)
                    for d in range(2, J + 1):
                        last = te.matmul(cum[:, d * NB:(J + 1) * NB], ones[:, :], h[:, 0:(J + 1 - d) * NB], start=False, stop=d == J)
                    last.then_inc(ranks, 1)
                    out = psum[:, 6 + k, 0:J * M]
                    pe.wait_ge(ef_out, t + 1)
                    if later:
                        pe.wait_ge(rec_ready, t - 1)
                    for q in range(2):
                        te.matmul(out[:, q * 2 * M:(q + 1) * 2 * M], eft[:, k, q * P:(q + 1) * P], w_ef[:, :], start=q == 0, stop=False)
                    pe.wait_ge(window, t + 1)
                    pe.wait_ge(bw_in[k], 16 * (i + 1))
                    for j in range(J):
                        for part in range(3):
                            last = te.matmul(out[:, j * M:(j + 1) * M], win[:, k, j * P:(j + 1) * P], bwin[:, k, part, :],
                                             start=False, stop=j == J - 1 and part == 2)
                    last.then_inc(pre, 1)

                spread(0, 0)
                in_pairs(pe, step)

            @block.scalar
            def _(act):
                def step(i, k):
                    t = 2 * i + k
                    later = not (isinstance(i, int) and i == 0)
                    act.wait_ge(ef_t, t + 1)
                    if later:
                        act.wait_ge(pre, t - 1)
                    nc.scalar.copy(eft[:, k, :], psum[:, k, 0:2 * P]).then_inc(ef_out, 1)
                    if later:
                        act.wait_ge(scattered[k], 16 * J * i)
                    nc.scalar.copy(rec[:, k, :, M:RW], lo_col[:, ds(t, 1), :].rearrange("p o j -> p j o")).then_inc(lo_ready, 1)
                in_pairs(act, step)

            @block.vector
            def _(dve):
                v = nc.vector

                def onehots(i, k):
                    if not exists(i, k):
                        return
                    t = 2 * i + k
                    later = not (isinstance(i, int) and i == 0)
                    dve.wait_ge(rel_bc, t + 1)
                    if later:
                        dve.wait_ge(pre, t - 1)
                    v.tensor_scalar(win[:, k, :], psum[:, 2 + k, :], match[:, 0:1], None, ALU.is_equal).then_inc(window, 1)
                    if later:
                        dve.wait_ge(ranks, t - 1)
                        dve.wait_ge(pos_ready, t - 1)
                    v.tensor_tensor(out=hot[:, k, :, :], in0=iota[:, 0:NB].unsqueeze(1).broadcast_to([P, J, NB]),
                                    in1=hi_col[:, ds(t, 1), :].rearrange("p o j -> p j o").broadcast_to([P, J, NB]),
                                    op=ALU.is_equal).then_inc(onehot, 1)

                def step(i, k):
                    t = 2 * i + k
                    later = not (isinstance(i, int) and i == 0)
                    onehots(*after(i, k))
                    cum = psum[:, 4 + k, :]
                    dve.wait_ge(ranks, t + 1)
                    if later or k:
                        dve.wait_ge(ranks_read, t)
                    v.tensor_tensor(out=s1[:, :, :], in0=cum[:, 0:J * NB].rearrange("p (j b) -> p j b", j=J),
                                    in1=base[:, :].unsqueeze(1).broadcast_to([P, J, NB]), op=ALU.add).then_inc(dve_p, 1)
                    dve.wait_ge(dve_p, 3 * t + 1)
                    v.tensor_tensor(out=base[:, :], in0=base[:, :], in1=cum[:, J * NB:(J + 1) * NB], op=ALU.add).then_inc(ranks_read, 1)
                    v.tensor_tensor(out=s2[:, :, :], in0=s1[:, :, :], in1=hot[:, k, :, :], op=ALU.mult).then_inc(dve_p, 1)
                    dve.wait_ge(pre, t + 1)
                    dve.wait_ge(gathered, t + 1)
                    if later:
                        dve.wait_ge(scattered[k], 16 * J * i)
                    v.tensor_tensor(out=rec[:, k, :, 0:M], in0=psum[:, 6 + k, 0:J * M].rearrange("p (j m) -> p j m", j=J),
                                    in1=gat[:, k, :, :], op=ALU.add).then_inc(rec_ready, 1)
                    dve.wait_ge(dve_p, 3 * t + 2)
                    v.tensor_reduce(out=pos_f[:, :], in_=s2[:, :, :], op=ALU.add, axis=AX).then_inc(dve_p, 1)
                    dve.wait_ge(dve_p, 3 * t + 3)
                    tail = isinstance(i, int) and t == NS - 1
                    ins = v.tensor_copy(pos[:, k, :], pos_f[:, :])
                    if tail:
                        ins.then_inc(tail_pos, 1)
                        dve.wait_ge(tail_pos, 1)
                        ins = v.memset(pos[0:SEEN, k, :], ROWS)
                    ins.then_inc(pos_ready, 1)

                onehots(0, 0)
                in_pairs(dve, step)

        acc = sb("acc", [P, FG * NG, M], f32)
        assert FG * NG > NB
        U = 2
        J2 = U * J
        BODY = 6
        STEPS = NS2 // U
        assert STEPS % BODY == 0
        rows_in = [sem(f"rows_in{q}") for q in range(BODY // 2)]
        acc_clear = sem("acc_clear")
        lo_hot = [sem("lo_hot_dve"), sem("lo_hot_pool")]
        hot_turns = sem("hot_turns")
        lo_hot_t, lo_hot_out = sem("lo_hot_t"), sem("lo_hot_out")
        a_mm, msg_sum, msg_h, msg_r = sem("a_mm"), sem("msg_sum"), sem("msg_h"), sem("msg_r")
        msg_m, msg_l, sum_mm, acc_first, acc_second = sem("msg_m"), sem("msg_l"), sem("sum_mm"), sem("acc_first"), sem("acc_second")
        with ExitStack() as tmp:
            rec2 = sb("rec2", [P, BODY, U, J, RW], f32, tmp)
            lhot = sb("lhot", [P, BODY, J2, P], bf16, tmp)
            lhot_t = sb("lhot_t", [P, 2, J2, P], bf16, tmp)
            msg = sb("msg", [P, 2, J2, M], f32, tmp)
            msgr = sb("msgr", [P, 2, J2, M], f32, tmp)
            msgp = sb("msgp", [P, BODY, 3, J2, M], bf16, tmp)
            block = tmp.enter_context(nc.Block())

            def shift(g, k, n):
                return g + (k + n) // BODY, (k + n) % BODY

            def inside(g, k):
                return not isinstance(g, int) or 0 <= BODY * g + k < STEPS

            def from_(g, k, n):
                return not isinstance(g, int) or BODY * g + k >= n

            def in_bodies(eng, step):
                last = STEPS // BODY - 1
                for g in (-1, 0):
                    for k in range(BODY):
                        step(g, k)
                with eng.Fori(1, last) as g:
                    for k in range(BODY):
                        step(g, k)
                for g in (last, last + 1):
                    for k in range(BODY):
                        step(g, k)

            @block.sync
            def _(sp):
                def load(g, q, later):
                    if later:
                        sp.wait_ge(msg_sum, BODY * (g - 1) + 2 * q + 2)
                    sp.dma_start(rec2[:, 2 * q:2 * q + 2, :, :, :].rearrange("p a u j w -> p (a u) (j w)"),
                                 rows[ds((g * (BODY // 2) + q) * (2 * U * T), 2 * U * T), :].rearrange("(s p j) w -> p s (j w)", p=P, j=J))\
                        .then_inc(rows_in[q], 16)
                for q in range(BODY // 2):
                    load(0, q, False)
                with sp.Fori(1, STEPS // BODY) as g:
                    for q in range(BODY // 2):
                        load(g, q, True)

            POOLS = 2

            def before_one_hot(eng, g, k):
                if k % 2 == 0:
                    eng.wait_ge(rows_in[k // 2], 16 * (g + 1))
                if from_(g, k, BODY):
                    eng.wait_ge(sum_mm, BODY * g + k - BODY + 1)

            def numbers(k):
                return rec2[:, k, :, :, M:RW].rearrange("p u j o -> p (u j) o")

            @block.gpsimd
            def _(pool):
                pool.memset(acc[:, :, :], 0.0).then_inc(acc_clear, 1)

                def step(g, k):
                    ahead = shift(g, k, 2)
                    if inside(*ahead):
                        before_one_hot(pool, *ahead)
                        pool.sem_inc(hot_turns, 1)
                        for j in range(J2 - POOLS, J2):
                            last = pool.tensor_scalar(lhot[:, ahead[1], j, :], iota[:, :], numbers(ahead[1])[:, j, :], None, ALU.is_equal)
                        last.then_inc(lo_hot[1], 1)
                    if inside(*shift(g, k, -2)):
                        q = (k - 2) % BODY
                        pool.wait_ge(msg_m, BODY * g + k - 1)
                        pool.tensor_tensor(out=msgp[:, q, 2, :, :], in0=msgr[:, q % 2, :, :], in1=msgp[:, q, 1, :, :],
                                           op=ALU.subtract).then_inc(msg_l, 1)
                in_bodies(pool, step)

            @block.tensor
            def _(pe):
                te = nc.tensor
                bucket = [pe.alloc_register(f"pe_bucket{u}") for u in range(U)]

                def turn(g, k):
                    if not inside(g, k):
                        return
                    s = BODY * g + k
                    for made in lo_hot:
                        pe.wait_ge(made, s + 1)
                    if from_(g, k, 2):
                        pe.wait_ge(lo_hot_out, s - 1)
                    for j in range(J2):
                        last = te.transpose(psumb[:, k % 2, j * P:(j + 1) * P], lhot[:, k, j, :], ident[:, :])
                    last.then_inc(lo_hot_t, 1)

                def add_a(g, k, bs):
                    s = BODY * g + k
                    pe.wait_ge(lo_hot_out, s + 1)
                    if from_(g, k, 2):
                        pe.wait_ge(msg_sum, s - 1)
                    for j in range(J2):
                        for part in range(3):
                            last = te.matmul(psum[:, 2 + k % 2, j * M:(j + 1) * M], lhot_t[:, k % 2, j, :],
                                             a_tab[:, ds(bs[j // J], 1), part, :].rearrange("p o m -> p (o m)"),
                                             start=j == 0 and part == 0, stop=j == J2 - 1 and part == 2)
                    last.then_inc(a_mm, 1)

                def sum_up(g, k):
                    if not inside(g, k):
                        return
                    s = BODY * g + k
                    pe.wait_ge(msg_l, s + 1)
                    if from_(g, k, 2):
                        pe.wait_ge(acc_second, s - 1)
                    for j in range(J2):
                        u = j // J
                        for part in range(3):
                            last = te.matmul(psum[:, 4 + k % 2, u * M:(u + 1) * M], lhot[:, k, j, :], msgp[:, k, part, j, :],
                                             start=j == 0 and part == 0, stop=j == J2 - 1 and part == 2)
                    last.then_inc(sum_mm, 1)

                def step(g, k):
                    if inside(g, k):
                        pe.load(bucket, bucket_row[0:1, ds((BODY * g + k) * U, U)])
                        bs = [pe.snap(b, min_val=0, max_val=SPARE) for b in bucket]
                    turn(*shift(g, k, 1))
                    if inside(g, k):
                        add_a(g, k, bs)
                    sum_up(*shift(g, k, -3))
                in_bodies(pe, step)

            @block.scalar
            def _(act):
                def step(g, k):
                    if inside(*shift(g, k, 1)):
                        s, q = BODY * g + k + 1, (k + 1) % 2
                        act.wait_ge(lo_hot_t, s + 1)
                        if from_(*shift(g, k, 1), 2):
                            act.wait_ge(a_mm, s - 1)
                        nc.scalar.copy(lhot_t[:, q, :, :].rearrange("p j e -> p (j e)"), psumb[:, q, 0:J2 * P]).then_inc(lo_hot_out, 1)
                    if inside(*shift(g, k, -1)):
                        q = (k - 1) % BODY
                        act.wait_ge(msg_r, BODY * g + k)
                        nc.scalar.copy(msgp[:, q, 1, :, :], msgr[:, q % 2, :, :]).then_inc(msg_m, 1)
                    if inside(g, k):
                        s = BODY * g + k
                        act.wait_ge(msg_sum, s + 1)
                        if from_(g, k, BODY):
                            act.wait_ge(sum_mm, s - BODY + 1)
                        nc.scalar.activation(msgp[:, k, 0, :, :], msg[:, k % 2, :, :], ACT.Relu).then_inc(msg_h, 1)
                in_bodies(act, step)

            @block.vector
            def _(dve):
                v = nc.vector
                bucket = [dve.alloc_register(f"dve_bucket{u}") for u in range(U)]
                dve.wait_ge(acc_clear, 1)

                def add_sum(k, bs, u, signal):
                    a = acc[:, ds(bs[u], 1), :].rearrange("p o m -> p (o m)")
                    v.tensor_tensor(out=a, in0=a, in1=psum[:, 4 + k % 2, u * M:(u + 1) * M], op=ALU.add).then_inc(signal, 1)

                def flat(t):
                    return t.rearrange("p j m -> p (j m)")

                def step(g, k):
                    s = BODY * g + k
                    done = inside(*shift(g, k, -4))
                    if done:
                        dve.load(bucket, bucket_row[0:1, ds((s - 4) * U, U)])
                        bs = [dve.snap(b, min_val=0, max_val=SPARE) for b in bucket]
                    ahead = shift(g, k, 2)
                    if inside(*ahead):
                        before_one_hot(dve, *ahead)
                        n = J2 - POOLS
                        v.tensor_tensor(out=lhot[:, ahead[1], 0:n, :], in0=iota[:, :].unsqueeze(1).broadcast_to([P, n, P]),
                                        in1=numbers(ahead[1])[:, 0:n, :].broadcast_to([P, n, P]), op=ALU.is_equal).then_inc(lo_hot[0], 1)
                    if inside(*shift(g, k, -1)):
                        q = (k - 1) % BODY
                        dve.wait_ge(msg_h, s)
                        if from_(g, k, 3):
                            dve.wait_ge(msg_l, s - 2)
                        v.scalar_tensor_tensor(out=flat(msgr[:, q % 2, :, :]), in0=flat(msg[:, q % 2, :, :]), scalar=0.0,
                                               in1=flat(msgp[:, q, 0, :, :]), op0=ALU.max, op1=ALU.subtract).then_inc(msg_r, 1)
                    if done:
                        dve.wait_ge(sum_mm, s - 3)
                        if from_(g, k, 5):
                            dve.wait_ge(acc_second, s - 4)
                        add_sum(k, bs, 0, acc_first)
                    if inside(g, k):
                        dve.wait_ge(a_mm, s + 1)
                        if from_(g, k, 2):
                            dve.wait_ge(msg_r, s - 1)
                        v.tensor_tensor(out=msg[:, k % 2, :, :], in0=psum[:, 2 + k % 2, 0:J2 * M].rearrange("p (j m) -> p j m", j=J2),
                                        in1=rec2[:, k, :, :, 0:M].rearrange("p u j m -> p (u j) m"), op=ALU.add).then_inc(msg_sum, 1)
                    if done:
                        dve.wait_ge(acc_first, s - 3)
                        add_sum(k, bs, 1, acc_second)
                in_bodies(dve, step)

        x_again, sums_t, sums_out, y_mm = sem("x_again"), sem("sums_t"), sem("sums_out"), sem("y_mm")
        z_ready, y_ready, y_out, x_free = sem("z_ready"), sem("y_ready"), sem("y_out"), sem("x_free")
        with ExitStack() as tmp:
            xf = sb("xf", [P, NG, FG, F], f32, tmp)
            st = sb("st", [P, 2, P], f32, tmp)
            z = sb("z", [P, 2, FG * F], f32, tmp)
            LB = NB - (NG - 1) * FG
            x_clear = sem("x_clear")
            cp = sb("cp", [P, 2, P], f32, tmp)
            sums_cp = sem("sums_cp")
            assert NG % 2 == 1

            def finish(eng, step):
                for k in range(2):
                    step(k, k, FG)
                with eng.Fori(1, NG // 2) as i:
                    for k in range(2):
                        step(2 * i + k, k, FG)
                step(NG - 1, 0, LB)

            block = tmp.enter_context(nc.Block())

            @block.sync
            def _(sp):
                main = (NB - 1) * P
                xb_ = xf[:, :, :, :].rearrange("p g q f -> p (g q) f")
                sp.dma_start(xb_[:, 0:NB - 1, :], x[0:main, :].rearrange("(b p) f -> p b f", p=P)).then_inc(x_again, 16)
                sp.wait_ge(x_clear, 1)
                sp.dma_start(xb_[0:NTAIL, NB - 1, :], x[main:N, :]).then_inc(x_again, 16)
                with sp.Fori(0, NG - 1) as g:
                    sp.wait_ge(y_ready, g + 1)
                    sp.dma_start(y[ds(g * (FG * P), FG * P), :].rearrange("(q p) f -> p q f", p=P),
                                 xf[:, ds(g, 1), :, :].rearrange("p o q f -> p (o q) f")).then_inc(y_out, 16)
                sp.wait_ge(y_ready, NG)
                r0 = (NG - 1) * FG * P
                sp.dma_start(y[r0:main, :].rearrange("(q p) f -> p q f", p=P), xf[:, NG - 1, 0:LB - 1, :]).then_inc(y_out, 16)
                sp.dma_start(y[main:N, :], xf[0:NTAIL, NG - 1, LB - 1, :]).then_inc(y_out, 16)
                sp.wait_ge(y_out, 16 * (NG + 1))

            @block.gpsimd
            def _(pool):
                pool.memset(xf[:, NG - 1, LB - 1, :], 0.0).then_inc(x_clear, 1)

            @block.tensor
            def _(pe):
                def step(g, k, nb):
                    later = not (isinstance(g, int) and g < 2)
                    pe.wait_ge(sums_cp, g + 1)
                    if later:
                        pe.wait_ge(sums_out, g - 1)
                    nc.tensor.transpose(psum[:, k, 0:P], cp[:, k, :], identf[:, :]).then_inc(sums_t, 1)
                    pe.wait_ge(sums_out, g + 1)
                    if later:
                        pe.wait_ge(z_ready, g - 1)
                    nc.tensor.matmul(psum[:, 2 + k, 0:nb * F], st[:, k, :],
                                     w_sum[:, 0:nb, :].rearrange("p q f -> p (q f)"), start=True, stop=True).then_inc(y_mm, 1)
                finish(pe, step)

            @block.scalar
            def _(act):
                def copy(g, k):
                    later = not (isinstance(g, int) and g < 2)
                    if later:
                        act.wait_ge(sums_t, g - 1)
                    nc.scalar.copy(cp[:, k, :], acc[:, ds(g * FG, FG), :].rearrange("p q m -> p (q m)")).then_inc(sums_cp, 1)

                def step(g, k, nb):
                    later = not (isinstance(g, int) and g < 2)
                    copy(g, k)
                    act.wait_ge(sums_t, g + 1)
                    if later:
                        act.wait_ge(y_mm, g - 1)
                    nc.scalar.copy(st[:, k, :], psum[:, k, 0:P]).then_inc(sums_out, 1)
                finish(act, step)

            @block.vector
            def _(dve):
                v = nc.vector
                dve.wait_ge(x_again, 32)

                def step(g, k, nb):
                    later = not (isinstance(g, int) and g < 2)
                    dve.wait_ge(y_mm, g + 1)
                    if later:
                        dve.wait_ge(y_ready, g - 1)
                    v.tensor_tensor(out=z[:, k, 0:nb * F], in0=psum[:, 2 + k, 0:nb * F],
                                    in1=ypart[:, ds(g * FG, nb), :].rearrange("p q f -> p (q f)"), op=ALU.add).then_inc(z_ready, 1)
                    dve.wait_ge(z_ready, g + 1)
                    xg = xf[:, ds(g, 1), 0:nb, :].rearrange("p o q f -> p (o q f)")
                    v.scalar_tensor_tensor(out=xg, in0=z[:, k, 0:nb * F], scalar=0.0, in1=xg, op0=ALU.max, op1=ALU.add)\
                        .then_inc(y_ready, 1)
                finish(dve, step)


def kernel(x, src, dst, edge_attr_64, L0_gnn_W_edge, L0_gnn_b_edge, L0_gnn_W_node, L0_gnn_b_node):
    import numpy as np
    import concourse.bacc as bacc
    from concourse import mybir as mb
    from concourse.bass_utils import run_bass_kernel_spmd

    ins = {"x": x, "src": src, "dst": dst, "edge_attr": edge_attr_64, "w_edge": L0_gnn_W_edge,
           "b_edge": L0_gnn_b_edge, "w_node": L0_gnn_W_node, "b_node": L0_gnn_b_node}
    nc = bacc.Bacc("TRN2", target_bir_lowering=False, num_devices=1)
    arrays, aps = {}, []
    for name, a in ins.items():
        a = np.ascontiguousarray(a)
        arrays[name] = a
        aps.append(nc.dram_tensor(name, a.shape, mb.dt.from_np(a.dtype), kind="ExternalInput").ap())
    out = nc.dram_tensor("y", tuple(x.shape), mb.dt.float32, kind="ExternalOutput").ap()
    gnn_layer(nc, *aps, out)
    r = run_bass_kernel_spmd(nc, [arrays], core_ids=[0])
    return r.results[0]["y"]
```

```python
import concourse.bass as bass
from concourse import mybir
from contextlib import ExitStack


def gnn_layer(nc, x, src, dst, ef, w_edge, b_edge, w_node, b_node, y):
    f32, bf16, i32 = mybir.dt.float32, mybir.dt.bfloat16, mybir.dt.int32
    ALU = mybir.AluOpType
    ACT = mybir.ActivationFunctionType
    AX = mybir.AxisListType.X
    ds = bass.ds

    P = 128
    N, F = x.shape
    E, FE = ef.shape
    M = w_edge.shape[1]
    J = 4
    T = P * J
    NS = -(-E // T)
    LAST0 = E - T
    SEEN = (NS * T - E) // J
    assert (NS * T - E) % J == 0 and NS % 2 == 0
    SB = -(-NS // P)
    assert SB % 2 == 1 and SB >= 3
    NB = -(-N // P)
    NTAIL = N - (NB - 1) * P
    BODY, U = 8, 2
    NS2 = -(-(E // T + NB + 1) // (BODY * U)) * (BODY * U)
    assert NS2 * T >= E + NB * (T - 1)
    ROWS = NS2 * T
    RW = M + 1
    SPARE = NB
    DG = 8
    DU = NB // DG + 1
    GC = 8
    DV = DU + DG
    assert DU * GC <= P and DU * DG > NB and DU * DG <= P
    CB = 14
    NC = NB // CB
    assert NC * CB == NB
    WC = F + 2 * M
    FG = 4
    NG = -(-NB // FG)

    rows = nc.dram_tensor("edge_rows", (ROWS, RW), f32, kind="Internal").ap()
    b_parts = nc.dram_tensor("b_parts", ((NB + 1) * P, 3 * M), bf16, kind="Internal").ap()
    b_rows = nc.dram_tensor("b_rows", (NB * P, M), f32, kind="Internal").ap()
    bucket_dram = nc.dram_tensor("bucket_of", (1, P * 8), i32, kind="Internal").ap()

    ctx = ExitStack()
    with ctx:
        def sb(name, shape, dt, where=ctx):
            return where.enter_context(nc.sbuf_tensor(name, shape, dt))

        def sem(name):
            return ctx.enter_context(nc.semaphore(name))

        psum = ctx.enter_context(nc.psum_tensor("psum", [P, 8, 512], f32))
        psumb = psum[:, :, :].bitcast(bf16)

        ident = sb("ident", [P, P], bf16)
        identf = sb("identf", [P, P], f32)
        ones = sb("ones", [P, P], bf16)
        onesf = sb("onesf", [P, P], f32)
        upper = sb("upper", [P, P], bf16)
        iota_i = sb("iota_i", [P, P], i32)
        part_i = sb("part_i", [P, 1], i32)
        sidx_i = sb("sidx_i", [P, 8], i32)
        iota = sb("iota", [P, P], bf16)
        iotaf = sb("iotaf", [P, P], f32)
        partf = sb("partf", [P, 1], f32)
        sidx = sb("sidx", [P, 8], f32)
        eps = sb("eps", [P, 1], f32)
        PR = 64
        PIECES = T // PR
        filler = sb("filler", [P, PR * RW], f32)
        wcat = sb("wcat", [P, WC], f32)
        bias = sb("bias", [P, WC], f32)
        w_ef = sb("w_ef", [P, 2 * M], f32)
        w_sum = sb("w_sum", [P, FG, F], f32)
        base = sb("base", [P, NB], f32)
        match = sb("match", [P, 1], f32)
        general_i = sb("general_i", [P, 1], i32)
        last_i = sb("last_i", [P, PIECES], i32)
        bucket_row = sb("bucket_row", [1, P * 8], i32)
        a_tab = sb("a_tab", [P, NB + 1, 3, M], bf16)
        ypart = sb("ypart", [P, NB, F], f32)

        edges = ctx.enter_context(ExitStack())
        hi_col = sb("hi_col", [P, SB * P, J], bf16, edges)
        lo_col = sb("lo_col", [P, SB * P, J], bf16, edges)
        dst_col = sb("dst_col", [P, SB * P, J], i32, edges)
        rel_row = sb("rel_row", [P, SB, T], bf16, edges)

        consts, cast = sem("consts"), sem("cast")
        weights_in, idx_in, idx_clear = sem("weights_in"), sem("idx_in"), sem("idx_clear")
        w_clear = sem("w_clear")
        end_filled, last_filled = sem("end_filled"), sem("last_filled")
        dve_e, cols_t, cols_out = sem("dve_e"), sem("cols_t"), sem("cols_out")
        idx_rows, viol_ready, counted, buckets_ready = sem("idx_rows"), sem("viol_ready"), sem("counted"), sem("buckets_ready")
        dcols_out, count_mm, flag_mm = sem("dcols_out"), sem("count_mm"), sem("flag_mm")
        low_steps, digits_ready, digits_mm = sem("low_steps"), sem("digits_ready"), sem("digits_mm")
        bucket_out, bucket_in = sem("bucket_out"), sem("bucket_in")
        last_ready = sem("last_ready")
        with ExitStack() as tmp:
            src_row = sb("src_row", [P, SB, T], i32, tmp)
            dst_row = sb("dst_row", [P, SB, T], i32, tmp)
            t1 = sb("t1", [P, SB, T], i32, tmp)
            t2 = sb("t2", [P, SB, T], i32, tmp)
            hi_row = sb("hi_row", [P, SB, T], bf16, tmp)
            lo_row = sb("lo_row", [P, SB, T], bf16, tmp)
            spans = sb("spans", [P, 4, SB], f32, tmp)
            viol = sb("viol", [P, 1], f32, tmp)
            violb = sb("violb", [P, 1], bf16, tmp)
            low = sb("low", [P, T], bf16, tmp)
            digits = ypart[:, :, :].bitcast(bf16).rearrange("p b f -> p (b f)")[:, 0:2 * DV * T]\
                .rearrange("p (k g v c) -> p k g v c", k=2, v=DV, c=GC)
            digit_i = sb("digit_i", [P, 4, P], i32, tmp)
            digit_f = sb("digit_f", [P, 4, P], f32, tmp)
            same_col = sb("same_col", [P, P], f32, tmp)
            upper_is = sb("upper_is", [P, P], f32, tmp)
            upper_next = sb("upper_next", [P, P], f32, tmp)
            pairs = sb("pairs", [P, DG * GC], f32, tmp)
            pair_sum = sb("pair_sum", [P, DG], f32, tmp)
            spread_sum = sb("spread_sum", [P, DU, DG], f32, tmp)
            c_f = sb("c_f", [P, 3, NB], f32, tmp)
            c_i = sb("c_i", [P, 2, NB], i32, tmp)
            last_f = sb("last_f", [P, NB + 2], f32, tmp)
            cmp = sb("cmp", [P, 8, NB], f32, tmp)
            bk_f = sb("bk_f", [P, 8], f32, tmp)
            bk_i = sb("bk_i", [P, 8], i32, tmp)
            REST = NS - 1 - (SB - 1) * P
            block = tmp.enter_context(nc.Block())

            @block.sync
            def _(sp):
                full = (SB - 1) * P * T
                for row, arr in ((src_row, src), (dst_row, dst)):
                    sp.dma_start(row[:, 0:SB - 1, :], arr[0:full].rearrange("(b s e) -> s b e", s=P, e=T)).then_inc(idx_in, 16)
                sp.wait_ge(idx_clear, 2)
                for row, arr in ((src_row, src), (dst_row, dst)):
                    sp.dma_start(row[0:REST, SB - 1, :], arr[full:full + REST * T].rearrange("(s e) -> s e", e=T)).then_inc(idx_in, 16)
                    sp.dma_start(row[REST:REST + 1, SB - 1, :], arr[LAST0:E].rearrange("(s e) -> s e", e=T)).then_inc(idx_in, 16)
                sp.wait_ge(buckets_ready, 1)
                sp.dma_start(bucket_dram.rearrange("o (p c) -> (o p) c", c=8), bk_i[:, :]).then_inc(bucket_out, 16)
                sp.wait_ge(bucket_out, 16)
                sp.dma_start(bucket_row[:, :], bucket_dram).then_inc(bucket_in, 16)
                sp.wait_ge(bucket_in, 16)

            @block.gpsimd
            def _(pool):
                pool.memset(src_row[:, SB - 1, :], 0).then_inc(idx_clear, 1)
                pool.memset(dst_row[:, SB - 1, :], 0).then_inc(idx_clear, 1)
                pool.memset(filler[:, :], -1.0).then_inc(consts, 1)
                pool.memset(w_ef[:, :], 0.0).then_inc(w_clear, 1)
                pool.memset(w_sum[:, :, :], 0.0).then_inc(w_clear, 1)
                pool.memset(bias[:, F:F + M], 0.0).then_inc(w_clear, 1)
                pool.memset(ones[:, :], 1.0).then_inc(consts, 1)
                pool.memset(onesf[:, :], 1.0).then_inc(consts, 1)
                pool.memset(eps[:, :], 1e-5).then_inc(consts, 1)
                pool.memset(ident[:, :], 0.0).then_inc(consts, 1)
                pool.memset(identf[:, :], 0.0).then_inc(consts, 1)
                pool.iota(iota_i[:, :], pattern=[[1, P]], base=0, channel_multiplier=0).then_inc(consts, 1)
                pool.iota(part_i[:, :], pattern=[[0, 1]], base=0, channel_multiplier=1).then_inc(consts, 1)
                pool.iota(sidx_i[:, :], pattern=[[1, 8]], base=0, channel_multiplier=8).then_inc(consts, 1)
                pool.wait_ge(consts, 9)
                for m in (ident, identf):
                    pool.affine_select(out=m[:, :], in_=m[:, :], compare_op=ALU.not_equal, fill=1.0, base=0,
                                       pattern=[[-1, P]], channel_multiplier=1).then_inc(consts, 1)
                pool.affine_select(out=upper[:, :], in_=ones[:, :], compare_op=ALU.is_gt, fill=0.0, base=0,
                                   pattern=[[1, P]], channel_multiplier=-1).then_inc(consts, 1)
                pool.wait_ge(last_ready, 1)
                pool.wait_ge(end_filled, 16 * 2)
                for q in range(PIECES):
                    pool.indirect_dma_start(out=rows.rearrange("(u r) w -> u (r w)", r=PR),
                                            out_offset=bass.IndirectOffsetOnAxis(ap=last_i[0:NB, q:q + 1], axis=0),
                                            in_=filler[0:NB, :], in_offset=None,
                                            bounds_check=ROWS // PR - 1, oob_is_err=False).then_inc(last_filled, 16)

            @block.vector
            def _(dve):
                n = [0]

                def link(ins, signal=None):
                    if signal is not None:
                        ins.then_inc(signal, 1)
                        dve.wait_ge(signal, 1)
                        return
                    n[0] += 1
                    ins.then_inc(dve_e, 1)
                    dve.wait_ge(dve_e, n[0])

                v = nc.vector
                dve.wait_ge(consts, 12)
                v.tensor_copy(iota[:, :], iota_i[:, :]).then_inc(cast, 1)
                v.tensor_copy(iotaf[:, :], iota_i[:, :]).then_inc(cast, 1)
                v.tensor_copy(partf[:, :], part_i[:, :]).then_inc(cast, 1)
                v.tensor_copy(sidx[:, :], sidx_i[:, :]).then_inc(cast, 1)
                dve.wait_ge(idx_in, 16 * 6)
                link(v.tensor_single_scalar(t1[:, :, :], src_row[:, :, :], P.bit_length() - 1, ALU.arith_shift_right))
                link(v.tensor_single_scalar(t2[:, :, :], src_row[:, :, :], P - 1, ALU.bitwise_and))
                link(v.tensor_copy(hi_row[:, :, :], t1[:, :, :]))
                link(v.tensor_copy(lo_row[:, :, :], t2[:, :, :]))
                dst_f, rel = t1[:, :, :].bitcast(f32), t2[:, :, :].bitcast(f32)
                link(v.tensor_copy(dst_f, dst_row[:, :, :]), idx_rows)
                link(v.tensor_tensor(out=rel, in0=dst_f, in1=dst_f[:, :, 0:1].broadcast_to([P, SB, T]), op=ALU.subtract))
                for b in range(SB):
                    link(v.tensor_copy(rel_row[:, b, :].rearrange("s (j p) -> s p j", j=J),
                                       rel[:, b, :].rearrange("s (p j) -> s p j", j=J)))
                link(v.tensor_reduce(out=spans[:, 0, :], in_=rel, op=ALU.max, axis=AX))
                link(v.tensor_reduce(out=spans[:, 1, :], in_=rel, op=ALU.min, axis=AX))
                link(v.tensor_single_scalar(spans[:, 2, :], spans[:, 0, :], float(P), ALU.is_ge))
                link(v.tensor_single_scalar(spans[:, 3, :], spans[:, 1, :], 0.0, ALU.is_lt))
                link(v.tensor_reduce(out=viol[:, :], in_=spans[:, 2:4, :].rearrange("p a b -> p (a b)"), op=ALU.add, axis=AX))
                link(v.tensor_copy(violb[:, :], viol[:, :]), viol_ready)
                for b in range(SB):
                    dve.wait_ge(cols_t, b + 1)
                    v.tensor_copy(dst_col[:, b * P:(b + 1) * P, :],
                                  psum[:, 4 + b % 2, :].rearrange("p (j s) -> p s j", j=J)).then_inc(dcols_out, 1)
                dve.wait_ge(flag_mm, 1)
                link(v.tensor_scalar(viol[:, :], psum[:, 6, 0:1], 1.0, None, ALU.min))
                link(v.tensor_copy(general_i[:, :], viol[:, :]))
                link(v.scalar_tensor_tensor(out=match[:, :], in0=viol[:, :], scalar=0.5, in1=partf[:, :], op0=ALU.mult, op1=ALU.add))
                link(v.tensor_single_scalar(digit_i[:, 0, 0:1], part_i[:, :], GC.bit_length() - 1, ALU.arith_shift_right))
                link(v.tensor_single_scalar(digit_i[:, 1, 0:1], part_i[:, :], GC - 1, ALU.bitwise_and))
                link(v.tensor_single_scalar(digit_i[:, 2, :], iota_i[:, :], DG.bit_length() - 1, ALU.arith_shift_right))
                link(v.tensor_single_scalar(digit_i[:, 3, :], iota_i[:, :], GC - 1, ALU.bitwise_and))
                link(v.tensor_copy(digit_f[:, 0:2, 0:1], digit_i[:, 0:2, 0:1]))
                link(v.tensor_copy(digit_f[:, 2:4, :], digit_i[:, 2:4, :]))
                link(v.tensor_scalar(same_col[:, :], digit_f[:, 3, :], digit_f[:, 1, 0:1], None, ALU.is_equal))
                link(v.tensor_scalar(upper_is[:, :], digit_f[:, 2, :], digit_f[:, 0, 0:1], None, ALU.is_equal))
                link(v.tensor_scalar(digit_f[:, 2, :], digit_f[:, 2, :], 1.0, None, ALU.add))
                link(v.tensor_scalar(upper_next[:, :], digit_f[:, 2, :], digit_f[:, 0, 0:1], None, ALU.is_equal))
                link(v.tensor_tensor(out=upper_is[:, :], in0=upper_is[:, :], in1=upper_next[:, :], op=ALU.subtract))

                def digits_of(b, k, last=False):
                    dve.wait_ge(cols_out, 2 * (b + 1))
                    if last:
                        v.memset(hi_col[0:SEEN, NS - 1, :], float(P - 1)).then_inc(low_steps, 1)
                        dve.wait_ge(low_steps, 3 * b + 1)
                        v.memset(hi_col[:, NS:SB * P, :], float(P - 1)).then_inc(low_steps, 1)
                        dve.wait_ge(low_steps, 3 * b + 2)
                    n = 2 * last
                    cols = hi_col[:, ds(b * P, P), :].rearrange("p s j -> p (s j)")
                    v.tensor_copy(t2[:, 0, :], cols).then_inc(low_steps, 1)
                    dve.wait_ge(low_steps, 3 * b + n + 1)
                    v.tensor_single_scalar(t2[:, 1, :], t2[:, 0, :], DG - 1, ALU.bitwise_and).then_inc(low_steps, 1)
                    dve.wait_ge(low_steps, 3 * b + n + 2)
                    v.tensor_copy(low[:, :], t2[:, 1, :]).then_inc(low_steps, 1)
                    if not isinstance(b, int) or b >= 2:
                        dve.wait_ge(digits_mm, b - 1)
                    grouped = cols.rearrange("p (g c) -> p g c", c=GC)
                    for d in range(DU):
                        v.tensor_scalar(digits[:, k, :, d, :], grouped, float(d * DG), None, ALU.is_ge)
                    dve.wait_ge(low_steps, 3 * b + n + 3)
                    for d in range(DG):
                        ins = v.tensor_scalar(digits[:, k, :, DU + d, :], low[:, :].rearrange("p (g c) -> p g c", c=GC),
                                              float(d), None, ALU.is_equal)
                    ins.then_inc(digits_ready, 1)

                digits_of(0, 0)
                digits_of(1, 1)
                with dve.Fori(1, SB // 2) as i:
                    for k in range(2):
                        digits_of(2 * i + k, k)
                digits_of(SB - 1, 0, last=True)
                rc = DU * GC
                dve.wait_ge(digits_mm, SB)
                link(v.tensor_tensor(out=pairs[0:rc, :], in0=psum[0:rc, 7, 0:DG * GC], in1=same_col[0:rc, 0:DG * GC], op=ALU.mult))
                link(v.tensor_reduce(out=pair_sum[0:rc, :], in_=pairs[0:rc, :].rearrange("p (d c) -> p d c", c=GC), op=ALU.add, axis=AX))
                link(v.tensor_tensor(out=spread_sum[0:rc, :, :], in0=pair_sum[0:rc, :].unsqueeze(1).broadcast_to([rc, DU, DG]),
                                     in1=upper_is[0:rc, 0:DU * DG].rearrange("p (u d) -> p u d", d=DG), op=ALU.mult), counted)
                dve.wait_ge(count_mm, 1)
                link(v.tensor_scalar(c_f[:, 0, :], psum[:, 6, 0:NB], float(T - 1), None, ALU.add))
                link(v.tensor_copy(c_i[:, 0, :], c_f[:, 0, :]))
                link(v.tensor_single_scalar(c_i[:, 1, :], c_i[:, 0, :], T.bit_length() - 1, ALU.arith_shift_right))
                link(v.tensor_copy(c_f[:, 0, :], c_i[:, 1, :]))
                link(v.tensor_tensor_scan(out=c_f[:, 1, :], data0=onesf[:, 0:NB], data1=c_f[:, 0, :], initial=0.0,
                                          op0=ALU.mult, op1=ALU.add))
                link(v.tensor_tensor(out=cmp[:, :, :], in0=c_f[:, 1:2, :].broadcast_to([P, 8, NB]),
                                     in1=sidx[:, :].unsqueeze(2).broadcast_to([P, 8, NB]), op=ALU.is_le))
                link(v.tensor_tensor(out=c_f[:, 2, :], in0=c_f[:, 1, :], in1=c_f[:, 0, :], op=ALU.subtract))
                link(v.tensor_scalar(base[:, :], c_f[:, 2, :], float(T), None, ALU.mult))
                link(v.tensor_reduce(out=bk_f[:, :], in_=cmp[:, :, :], op=ALU.add, axis=AX))
                link(v.tensor_copy(bk_i[:, :], bk_f[:, :]), buckets_ready)
                link(v.tensor_tensor(out=last_f[:, 0:NB], in0=c_f[:, 1, :], in1=identf[:, 0:NB], op=ALU.mult))
                link(v.tensor_reduce(out=last_f[:, NB:NB + 1], in_=last_f[:, 0:NB], op=ALU.add, axis=AX))
                link(v.tensor_scalar(last_f[:, NB + 1:NB + 2], last_f[:, NB:NB + 1], 1.0, -1.0, ALU.max, ALU.add))
                link(v.scalar_tensor_tensor(out=last_f[:, 0:PIECES], in0=last_f[:, NB + 1:NB + 2].broadcast_to([P, PIECES]),
                                            scalar=float(PIECES), in1=iotaf[:, 0:PIECES], op0=ALU.mult, op1=ALU.add))
                link(v.tensor_copy(last_i[:, :], last_f[:, 0:PIECES]), last_ready)

            @block.tensor
            def _(pe):
                pe.wait_ge(consts, 12)
                pe.wait_ge(idx_rows, 1)
                for b in range(SB):
                    if b >= 2:
                        pe.wait_ge(cols_out, 2 * (b - 1))
                        pe.wait_ge(dcols_out, b - 1)
                    for bank, row, idn in ((0, hi_row, ident), (2, lo_row, ident), (4, t1[:, :, :].bitcast(f32), identf)):
                        for j in range(J):
                            out = psum[:, 4 + b % 2, j * P:(j + 1) * P] if bank == 4 else psumb[:, bank + b % 2, j * P:(j + 1) * P]
                            last = nc.tensor.transpose(out, row[:, b, :].rearrange("s (p j) -> s j p", j=J)[:, j, :], idn[:, :])
                    last.then_inc(cols_t, 1)
                pe.wait_ge(viol_ready, 1)
                nc.tensor.matmul(psum[:, 6, 0:1], ones[:, :], violb[:, :], start=True, stop=True).then_inc(flag_mm, 1)

                def count(b, k, first=False, last_block=False):
                    pe.wait_ge(digits_ready, b + 1)
                    for g in range(T // GC):
                        last = nc.tensor.matmul(psum[0:DU * GC, 7, 0:DG * GC],
                                                digits[:, k, g, 0:DU, :].rearrange("p v c -> p (v c)"),
                                                digits[:, k, g, DU:DV, :].rearrange("p v c -> p (v c)"),
                                                start=first and g == 0, stop=last_block and g == T // GC - 1)
                    last.then_inc(digits_mm, 1)

                count(0, 0, first=True)
                count(1, 1)
                with pe.Fori(1, SB // 2) as i:
                    for k in range(2):
                        count(2 * i + k, k)
                count(SB - 1, 0, last_block=True)
                pe.wait_ge(counted, 1)
                nc.tensor.matmul(psum[:, 6, 0:DU * DG], onesf[0:DU * GC, :], spread_sum[0:DU * GC, :, :].rearrange("p u d -> p (u d)"),
                                 start=True, stop=True).then_inc(count_mm, 1)

            @block.scalar
            def _(act):
                act.wait_ge(w_clear, 3)
                act.dma_start(wcat[:, 0:F], w_node[0:F, :]).then_inc(weights_in, 16)
                act.dma_start(wcat[:, F:F + M], w_edge[0:F, :]).then_inc(weights_in, 16)
                act.dma_start(wcat[:, F + M:WC], w_edge[F:2 * F, :]).then_inc(weights_in, 16)
                for q in range(2):
                    act.dma_start(w_ef[q * FE:(q + 1) * FE, q * M:(q + 1) * M], w_edge[2 * F:2 * F + FE, :]).then_inc(weights_in, 16)
                for q in range(FG):
                    act.dma_start(w_sum[q * M:(q + 1) * M, q, :], w_node[F:F + M, :]).then_inc(weights_in, 16)
                act.dma_start(bias[:, 0:F], b_node.unsqueeze(0).broadcast_to([P, F])).then_inc(weights_in, 16)
                act.dma_start(bias[:, F + M:WC], b_edge.unsqueeze(0).broadcast_to([P, M])).then_inc(weights_in, 16)
                act.wait_ge(consts, 1)
                behind = rows[E // T * T:ROWS, :].rearrange("r c -> (r c)").rearrange("(p a) -> p a", p=P)
                reps = behind.shape[1] // (PR * RW)
                act.dma_start(behind[:, 0:reps * PR * RW].rearrange("p (a c) -> p a c", c=PR * RW),
                              filler[:, :].unsqueeze(1).broadcast_to([P, reps, PR * RW])).then_inc(end_filled, 16)
                act.dma_start(behind[:, reps * PR * RW:], filler[:, 0:behind.shape[1] - reps * PR * RW]).then_inc(end_filled, 16)
                for b in range(SB):
                    act.wait_ge(cols_t, b + 1)
                    for bank, col in ((0, hi_col), (2, lo_col)):
                        nc.scalar.copy(col[:, b * P:(b + 1) * P, :],
                                       psumb[:, bank + b % 2, 0:T].rearrange("p (j s) -> p s j", j=J)).then_inc(cols_out, 1)

        x_in = [sem("x_in0"), sem("x_in1")]
        pool_turns = sem("pool_turns")
        row_sum, mean, centred, sq_done = sem("row_sum"), sem("mean"), sem("centred"), sem("sq_done")
        sq_sum, std_done, inv_std = sem("sq_sum"), sem("std_done"), sem("inv_std")
        h_ready, ht_t, ht_out = sem("h_ready"), sem("ht_t"), sem("ht_out")
        node_mm, node_out = sem("node_mm"), sem("node_out")
        part_h, part_r, part_m, part_l = sem("part_h"), sem("part_r"), sem("part_m"), sem("part_l")
        rows_stored, parts_stored = sem("rows_stored"), sem("parts_stored")
        spare_clear, spare_out, tabs_done = sem("spare_clear"), sem("spare_out"), sem("tabs_done")
        with ExitStack() as tmp:
            NODE_BANKS = 4
            xb = sb("xb", [P, 2, CB, F], f32, tmp)
            xc = sb("xc", [P, CB, F], f32, tmp)
            sq = sb("sq", [P, CB, F], f32, tmp)
            hn = sb("hn", [P, CB, F], f32, tmp)
            ht = sb("ht", [P, 2, P], f32, tmp)
            stat = sb("stat", [P, 5, CB], f32, tmp)
            ab = sb("ab", [P, CB, 2 * M], f32, tmp)
            rest = sb("rest", [P, CB, 2 * M], f32, tmp)
            abp = sb("abp", [P, 3, CB, 2 * M], bf16, tmp)
            bst = sb("bst", [P, CB, 3, M], bf16, tmp)
            block = tmp.enter_context(nc.Block())

            def first(c):
                return isinstance(c, int) and c == 0

            def over_chunks(eng, step):
                step(0, True)
                with eng.Fori(1, NC - 1) as c:
                    step(c, True)
                step(NC - 1, False)

            @block.sync
            def _(sp):
                def load(c):
                    r0, k, n = c * (CB * P), c % 2, P if c < NC - 1 else NTAIL
                    sp.dma_start(xb[:, k, 0:CB - 1, :],
                                 x[ds(r0, (CB - 1) * P), :].rearrange("(b p) f -> p b f", p=P)).then_inc(x_in[k], 16)
                    sp.dma_start(xb[0:n, k, CB - 1, :], x[ds(r0 + (CB - 1) * P, n), :]).then_inc(x_in[k], 16)

                load(0)
                load(1)
                for c in range(NC):
                    if c + 2 < NC:
                        sp.wait_ge(centred, c + 1)
                        load(c + 2)
                    sp.wait_ge(node_out, (c + 1) * CB)
                    sp.dma_start(b_rows[ds(c * (CB * P), CB * P), :].rearrange("(b p) m -> p b m", p=P),
                                 ab[:, :, M:2 * M]).then_inc(rows_stored, 16)
                    sp.wait_ge(tabs_done, c + 1)
                    sp.dma_start(b_parts[ds(c * (CB * P), CB * P), :].rearrange("(b p) m -> p b m", p=P),
                                 bst[:, :, :, :].rearrange("p b t m -> p b (t m)")).then_inc(parts_stored, 16)
                sp.wait_ge(rows_stored, 16 * NC)
                sp.wait_ge(parts_stored, 16 * NC)

            @block.gpsimd
            def _(pool):
                pool.memset(a_tab[:, NB, :, :], 0.0).then_inc(spare_clear, 1)
                pool.memset(bst[:, 0, :, :], 0.0).then_inc(spare_clear, 1)
                pool.wait_ge(spare_clear, 2)
                pool.dma_start(b_parts[NB * P:(NB + 1) * P, :], bst[:, 0, :, :].rearrange("p t m -> p (t m)")).then_inc(spare_out, 16)
                pool.wait_ge(spare_out, 16)

                def tables(c, following):
                    pool.wait_ge(part_l, c + 1)
                    if not first(c):
                        pool.wait_ge(parts_stored, 16 * c)
                    pool.sem_inc(pool_turns, 1)
                    for t in range(3):
                        pool.tensor_copy(bst[:, :, t, :], abp[:, t, :, M:2 * M])
                        last = pool.tensor_copy(a_tab[:, ds(c * CB, CB), t, :], abp[:, t, :, 0:M])
                    last.then_inc(tabs_done, 1)
                over_chunks(pool, tables)

            @block.vector
            def _(dve):
                v = nc.vector

                def link(ins, signal, c):
                    ins.then_inc(signal, 1)
                    dve.wait_ge(signal, c + 1)

                def bc(i):
                    return stat[:, i, :].unsqueeze(2).broadcast_to([P, CB, F])

                def centre(c):
                    xs = xb[:, ds(c % 2, 1), :, :].rearrange("p o b f -> p (o b) f")
                    dve.wait_ge(x_in[0], 32 * ((c + 2) // 2))
                    if not first(c):
                        dve.wait_ge(x_in[1], 32 * ((c + 1) // 2))
                    link(v.tensor_reduce(out=stat[:, 0, :], in_=xs, op=ALU.add, axis=AX), row_sum, c)
                    link(v.tensor_scalar(stat[:, 1, :], stat[:, 0, :], 1.0 / F, None, ALU.mult), mean, c)
                    v.tensor_tensor(out=xc[:, :, :], in0=xs, in1=bc(1), op=ALU.subtract).then_inc(centred, 1)

                def square_sum(c):
                    dve.wait_ge(sq_done, c + 1)
                    v.tensor_reduce(out=stat[:, 2, :], in_=sq[:, :, :], op=ALU.add, axis=AX).then_inc(sq_sum, 1)

                def scale(c):
                    dve.wait_ge(std_done, c + 1)
                    link(v.reciprocal(stat[:, 4, :], stat[:, 3, :]), inv_std, c)
                    if not first(c):
                        dve.wait_ge(ht_t, c * CB)
                    v.tensor_tensor(out=hn[:, :, :], in0=xc[:, :, :], in1=bc(4), op=ALU.mult).then_inc(h_ready, 1)

                def chunk(c, following):
                    for b in range(CB):
                        dve.wait_ge(node_mm, c * CB + (b + 1))
                        bank = 2 + b % NODE_BANKS
                        v.tensor_tensor(out=ypart[:, ds(c * CB + b, 1), :].rearrange("p o f -> p (o f)"),
                                        in0=psum[:, bank, 0:F], in1=bias[:, 0:F], op=ALU.add)
                        if b == 0 and not first(c):
                            dve.wait_ge(rows_stored, 16 * c)
                        v.tensor_tensor(out=ab[:, b, :], in0=psum[:, bank, F:WC], in1=bias[:, F:WC], op=ALU.add)\
                            .then_inc(node_out, 1)
                        if following and b == 1:
                            centre(c + 1)
                        if following and b == CB // 2 + 1:
                            square_sum(c + 1)
                    if following:
                        scale(c + 1)
                    dve.wait_ge(part_h, c + 1)
                    link(v.tensor_tensor(out=rest[:, :, :], in0=ab[:, :, :], in1=abp[:, 0, :, :], op=ALU.subtract), part_r, c)
                    dve.wait_ge(part_m, c + 1)
                    v.tensor_tensor(out=abp[:, 2, :, :], in0=rest[:, :, :], in1=abp[:, 1, :, :], op=ALU.subtract).then_inc(part_l, 1)

                centre(0)
                square_sum(0)
                scale(0)
                over_chunks(dve, chunk)

            @block.tensor
            def _(pe):
                pe.wait_ge(weights_in, 16 * (5 + FG + 2))
                with pe.Fori(0, NC) as c:
                    pe.wait_ge(h_ready, c + 1)

                    def transpose(b):
                        if b >= 2:
                            pe.wait_ge(ht_out, c * CB + (b - 1))
                        nc.tensor.transpose(psum[:, b % 2, 0:P], hn[:, b, :], identf[:, :]).then_inc(ht_t, 1)

                    transpose(0)
                    for b in range(CB):
                        if b + 1 < CB:
                            transpose(b + 1)
                        pe.wait_ge(ht_out, c * CB + (b + 1))
                        if b >= NODE_BANKS:
                            pe.wait_ge(node_out, c * CB + (b + 1 - NODE_BANKS))
                        nc.tensor.matmul(psum[:, 2 + b % NODE_BANKS, 0:WC], ht[:, b % 2, :], wcat[:, :], start=True, stop=True)\
                            .then_inc(node_mm, 1)
                    pe.wait_ge(node_out, (c + 1) * CB)

            @block.scalar
            def _(act):
                a = nc.scalar

                def square(c):
                    act.wait_ge(centred, c + 1)
                    a.activation(sq[:, :, :], xc[:, :, :], ACT.Square).then_inc(sq_done, 1)

                def root(c):
                    act.wait_ge(sq_sum, c + 1)
                    a.activation(stat[:, 3, :], stat[:, 2, :], ACT.Sqrt, bias=eps[:, :], scale=1.0 / F).then_inc(std_done, 1)

                def chunk(c, following):
                    for b in range(CB):
                        act.wait_ge(ht_t, c * CB + (b + 1))
                        if b >= 2:
                            act.wait_ge(node_mm, c * CB + (b - 1))
                        a.activation(ht[:, b % 2, :], psum[:, b % 2, 0:P], ACT.Relu).then_inc(ht_out, 1)
                        if following and b == 4:
                            square(c + 1)
                    if following:
                        root(c + 1)
                    act.wait_ge(node_out, (c + 1) * CB)
                    if not first(c):
                        act.wait_ge(tabs_done, c)
                    a.copy(abp[:, 0, :, :], ab[:, :, :]).then_inc(part_h, 1)
                    act.wait_ge(part_r, c + 1)
                    a.copy(abp[:, 1, :, :], rest[:, :, :]).then_inc(part_m, 1)

                square(0)
                root(0)
                over_chunks(act, chunk)

        ef_in = [sem("ef_in0"), sem("ef_in1")]
        bw_in = [sem("bw_in0"), sem("bw_in1")]
        scattered = [sem("scattered0"), sem("scattered1")]
        gathered_dma, gathered, gidx_ready = sem("gathered_dma"), sem("gathered"), sem("gidx_ready")
        g_clear = sem("g_clear")
        ef_t, ef_out, rel_bc = sem("ef_t"), sem("ef_out"), sem("rel_bc")
        window, onehot, ranks, pre = sem("window"), sem("onehot"), sem("ranks"), sem("pre")
        dve_p, pos_ready, rec_ready, lo_ready = sem("dve_p"), sem("pos_ready"), sem("rec_ready"), sem("lo_ready")
        ranks_read, tail_pos = sem("ranks_read"), sem("tail_pos")
        with ExitStack() as tmp:
            eft_in = sb("eft_in", [P, 2, J, FE], f32, tmp)
            eft = sb("eft", [P, 2, 2 * P], f32, tmp)
            bwin = sb("bwin", [P, 2, 3, M], bf16, tmp)
            win = sb("win", [P, 2, T], bf16, tmp)
            hot = sb("hot", [P, 2, J, NB], bf16, tmp)
            s1 = sb("s1", [P, J, NB], f32, tmp)
            s2 = sb("s2", [P, J, NB], f32, tmp)
            pos_f = sb("pos_f", [P, J], f32, tmp)
            pos = sb("pos", [P, 2, J], i32, tmp)
            rec = sb("rec", [P, 2, J, RW], f32, tmp)
            gat = sb("gat", [P, 2, J, M], f32, tmp)
            gidx = sb("gidx", [P, 2, J], i32, tmp)
            block = tmp.enter_context(nc.Block())

            def in_pairs(eng, step):
                for k in range(2):
                    step(0, k)
                with eng.Fori(1, NS // 2 - 1) as i:
                    for k in range(2):
                        step(i, k)
                for k in range(2):
                    step(NS // 2 - 1, k)

            def after(i, k, n=1):
                return i + (k + n) // 2, (k + n) % 2

            def start_of(i, k):
                return LAST0 if isinstance(i, int) and 2 * i + k == NS - 1 else (2 * i + k) * T

            def exists(i, k):
                return not isinstance(i, int) or 0 <= 2 * i + k < NS

            @block.sync
            def _(sp):
                def step(i, k):
                    t, e0 = 2 * i + k, start_of(i, k)
                    later = not (isinstance(i, int) and i == 0)
                    if later:
                        sp.wait_ge(ef_t, t - 1)
                    sp.dma_start(eft_in[:, k, :, :].rearrange("p j f -> p (j f)"),
                                 ef[ds(e0, T), :].rearrange("(p j) f -> p (j f)", j=J)).then_inc(ef_in[k], 16)
                    first = sp.value_load(dst[ds(e0, 1)].rearrange("(a b) -> a b", a=1), min_val=0, max_val=N - 1)
                    if later:
                        sp.wait_ge(pre, t - 1)
                    sp.dma_start(bwin[:, k, :, :].rearrange("p t m -> p (t m)"), b_parts[ds(first, P), :]).then_inc(bw_in[k], 16)
                in_pairs(sp, step)

            @block.gpsimd
            def _(pool):
                pool.memset(gat[:, :, :, :], 0.0).then_inc(g_clear, 1)
                pool.wait_ge(g_clear, 1)
                pool.wait_ge(last_filled, 16 * PIECES)

                def step(i, k, general):
                    t = 2 * i + k
                    later = not (isinstance(i, int) and i == 0)
                    if general:
                        if later:
                            pool.wait_ge(rec_ready, t - 1)
                        pool.tensor_copy(gidx[:, k, :], dst_col[:, ds(t, 1), :].rearrange("p o j -> p (o j)")).then_inc(gidx_ready, 1)
                        pool.wait_ge(gidx_ready, t + 1)
                        pool.sem_inc(pool_turns, 1)
                        for j in range(J):
                            pool.indirect_dma_start(out=gat[:, k, j, :], out_offset=None, in_=b_rows[:, :],
                                                    in_offset=bass.IndirectOffsetOnAxis(ap=gidx[:, k, j:j + 1], axis=0))\
                                .then_inc(gathered_dma, 16)
                        pool.wait_ge(gathered_dma, 16 * J * (t + 1))
                        pool.sem_inc(gathered, 1)
                    pool.wait_ge(pos_ready, t + 1)
                    pool.wait_ge(lo_ready, t + 1)
                    pool.wait_ge(rec_ready, t + 1)
                    pool.sem_inc(pool_turns, 1)
                    for j in range(J):
                        pool.indirect_dma_start(out=rows[:, :], out_offset=bass.IndirectOffsetOnAxis(ap=pos[:, k, j:j + 1], axis=0),
                                                in_=rec[:, k, j, :], in_offset=None,
                                                bounds_check=ROWS - 1, oob_is_err=False).then_inc(scattered[k], 16)

                flag = pool.value_load(general_i[0:1, 0:1], min_val=0, max_val=1)
                with pool.If(flag != 0):
                    in_pairs(pool, lambda i, k: step(i, k, True))
                with pool.Else():
                    pool.sem_inc(gathered, NS)
                    in_pairs(pool, lambda i, k: step(i, k, False))
                for k in range(2):
                    pool.wait_ge(scattered[k], 16 * J * (NS // 2))

            @block.tensor
            def _(pe):
                te = nc.tensor

                def spread(i, k):
                    if not exists(i, k):
                        return
                    t = 2 * i + k
                    later = not (isinstance(i, int) and i == 0)
                    if later:
                        pe.wait_ge(ef_out, t - 1)
                    pe.wait_ge(ef_in[k], 16 * (i + 1))
                    for q in range(2):
                        last = te.transpose(psum[:, k, q * P:(q + 1) * P],
                                            eft_in[:, k, 2 * q:2 * q + 2, :].rearrange("p j f -> p (j f)"), identf[:, :])
                    last.then_inc(ef_t, 1)
                    if later:
                        pe.wait_ge(window, t - 1)
                    te.matmul(psum[:, 2 + k, :], ident[:, ds(t % P, 1)].broadcast_to([P, P]),
                              rel_row[:, ds(t // P, 1), :].rearrange("s o e -> s (o e)"), start=True, stop=True).then_inc(rel_bc, 1)

                def step(i, k):
                    t = 2 * i + k
                    later = not (isinstance(i, int) and i == 0)
                    spread(*after(i, k))
                    cum = psum[:, 4 + k, :]
                    h = hot[:, k, :, :].rearrange("p j b -> p (j b)")
                    pe.wait_ge(onehot, t + 1)
                    if later:
                        pe.wait_ge(ranks_read, t - 1)
                    te.matmul(cum[:, 0:J * NB], upper[:, :], h, start=True, stop=False)
                    te.matmul(cum[:, J * NB:(J + 1) * NB], ones[:, :], h[:, (J - 1) * NB:], start=False, stop=False)
                    te.matmul(cum[:, NB:J * NB], ones[:, :], h[:, 0:(J - 1) * NB], start=False, stop=False)
                    for d in range(2, J + 1):
                        last = te.matmul(cum[:, d * NB:(J + 1) * NB], ones[:, :], h[:, 0:(J + 1 - d) * NB], start=False, stop=d == J)
                    last.then_inc(ranks, 1)
                    out = psum[:, 6 + k, 0:J * M]
                    pe.wait_ge(ef_out, t + 1)
                    if later:
                        pe.wait_ge(rec_ready, t - 1)
                    for q in range(2):
                        te.matmul(out[:, q * 2 * M:(q + 1) * 2 * M], eft[:, k, q * P:(q + 1) * P], w_ef[:, :], start=q == 0, stop=False)
                    pe.wait_ge(window, t + 1)
                    pe.wait_ge(bw_in[k], 16 * (i + 1))
                    for j in range(J):
                        for part in range(3):
                            last = te.matmul(out[:, j * M:(j + 1) * M], win[:, k, j * P:(j + 1) * P], bwin[:, k, part, :],
                                             start=False, stop=j == J - 1 and part == 2)
                    last.then_inc(pre, 1)

                spread(0, 0)
                in_pairs(pe, step)

            @block.scalar
            def _(act):
                def step(i, k):
                    t = 2 * i + k
                    later = not (isinstance(i, int) and i == 0)
                    act.wait_ge(ef_t, t + 1)
                    if later:
                        act.wait_ge(pre, t - 1)
                    nc.scalar.copy(eft[:, k, :], psum[:, k, 0:2 * P]).then_inc(ef_out, 1)
                    if later:
                        act.wait_ge(scattered[k], 16 * J * i)
                    nc.scalar.copy(rec[:, k, :, M:RW], lo_col[:, ds(t, 1), :].rearrange("p o j -> p j o")).then_inc(lo_ready, 1)
                in_pairs(act, step)

            @block.vector
            def _(dve):
                v = nc.vector

                def onehots(i, k):
                    if not exists(i, k):
                        return
                    t = 2 * i + k
                    later = not (isinstance(i, int) and i == 0)
                    dve.wait_ge(rel_bc, t + 1)
                    if later:
                        dve.wait_ge(pre, t - 1)
                    v.tensor_scalar(win[:, k, :], psum[:, 2 + k, :], match[:, 0:1], None, ALU.is_equal).then_inc(window, 1)
                    if later:
                        dve.wait_ge(ranks, t - 1)
                        dve.wait_ge(pos_ready, t - 1)
                    v.tensor_tensor(out=hot[:, k, :, :], in0=iota[:, 0:NB].unsqueeze(1).broadcast_to([P, J, NB]),
                                    in1=hi_col[:, ds(t, 1), :].rearrange("p o j -> p j o").broadcast_to([P, J, NB]),
                                    op=ALU.is_equal).then_inc(onehot, 1)

                def step(i, k):
                    t = 2 * i + k
                    later = not (isinstance(i, int) and i == 0)
                    onehots(*after(i, k))
                    cum = psum[:, 4 + k, :]
                    dve.wait_ge(ranks, t + 1)
                    if later or k:
                        dve.wait_ge(ranks_read, t)
                    v.tensor_tensor(out=s1[:, :, :], in0=cum[:, 0:J * NB].rearrange("p (j b) -> p j b", j=J),
                                    in1=base[:, :].unsqueeze(1).broadcast_to([P, J, NB]), op=ALU.add).then_inc(dve_p, 1)
                    dve.wait_ge(dve_p, 3 * t + 1)
                    v.tensor_tensor(out=base[:, :], in0=base[:, :], in1=cum[:, J * NB:(J + 1) * NB], op=ALU.add).then_inc(ranks_read, 1)
                    v.tensor_tensor(out=s2[:, :, :], in0=s1[:, :, :], in1=hot[:, k, :, :], op=ALU.mult).then_inc(dve_p, 1)
                    dve.wait_ge(pre, t + 1)
                    dve.wait_ge(gathered, t + 1)
                    if later:
                        dve.wait_ge(scattered[k], 16 * J * i)
                    v.tensor_tensor(out=rec[:, k, :, 0:M], in0=psum[:, 6 + k, 0:J * M].rearrange("p (j m) -> p j m", j=J),
                                    in1=gat[:, k, :, :], op=ALU.add).then_inc(rec_ready, 1)
                    dve.wait_ge(dve_p, 3 * t + 2)
                    v.tensor_reduce(out=pos_f[:, :], in_=s2[:, :, :], op=ALU.add, axis=AX).then_inc(dve_p, 1)
                    dve.wait_ge(dve_p, 3 * t + 3)
                    tail = isinstance(i, int) and t == NS - 1
                    ins = v.tensor_copy(pos[:, k, :], pos_f[:, :])
                    if tail:
                        ins.then_inc(tail_pos, 1)
                        dve.wait_ge(tail_pos, 1)
                        ins = v.memset(pos[0:SEEN, k, :], ROWS)
                    ins.then_inc(pos_ready, 1)

                onehots(0, 0)
                in_pairs(dve, step)

        edges.close()
        acc = sb("acc", [P, FG * NG, M], f32)
        assert FG * NG > NB
        xf = sb("xf", [P, NG, FG, F], f32)
        LB = NB - (NG - 1) * FG
        x_clear, x_again = sem("x_clear"), sem("x_again")
        J2 = U * J
        STEPS = NS2 // U
        assert STEPS % BODY == 0
        HOLD = 4
        assert BODY % HOLD == 0 and 4 % HOLD == 0
        rows_in = [sem(f"rows_in{q}") for q in range(BODY // 2)]
        acc_clear = sem("acc_clear")
        lo_hot = [sem("lo_hot_dve"), sem("lo_hot_pool")]
        hot_turns = sem("hot_turns")
        lo_hot_t, lo_hot_out = sem("lo_hot_t"), sem("lo_hot_out")
        a_mm, msg_sum, msg_h, msg_r = sem("a_mm"), sem("msg_sum"), sem("msg_h"), sem("msg_r")
        msg_m, msg_l, sum_mm, acc_first, acc_second = sem("msg_m"), sem("msg_l"), sem("sum_mm"), sem("acc_first"), sem("acc_second")
        with ExitStack() as tmp:
            rec2 = sb("rec2", [P, BODY, U, J, RW], f32, tmp)
            lhot = sb("lhot", [P, BODY, J2, P], bf16, tmp)
            lhot_t = sb("lhot_t", [P, 2, J2, P], bf16, tmp)
            msg = sb("msg", [P, 2, J2, M], f32, tmp)
            msgr = sb("msgr", [P, 2, J2, M], f32, tmp)
            msgp = sb("msgp", [P, BODY, 3, J2, M], bf16, tmp)
            block = tmp.enter_context(nc.Block())

            def shift(g, k, n):
                return g + (k + n) // BODY, (k + n) % BODY

            def inside(g, k):
                return not isinstance(g, int) or 0 <= BODY * g + k < STEPS

            def from_(g, k, n):
                return not isinstance(g, int) or BODY * g + k >= n

            def in_bodies(eng, step):
                last = STEPS // BODY - 1
                for g in (-1, 0):
                    for k in range(BODY):
                        step(g, k)
                with eng.Fori(1, last) as g:
                    for k in range(BODY):
                        step(g, k)
                for g in (last, last + 1):
                    for k in range(BODY):
                        step(g, k)

            @block.sync
            def _(sp):
                def load(g, q, later):
                    if later:
                        sp.wait_ge(msg_sum, BODY * (g - 1) + 2 * q + 2)
                    sp.dma_start(rec2[:, 2 * q:2 * q + 2, :, :, :].rearrange("p a u j w -> p (a u) (j w)"),
                                 rows[ds((g * (BODY // 2) + q) * (2 * U * T), 2 * U * T), :].rearrange("(s p j) w -> p s (j w)", p=P, j=J))\
                        .then_inc(rows_in[q], 16)
                for q in range(BODY // 2):
                    load(0, q, False)
                main = (NB - 1) * P
                x_blocks = xf[:, :, :, :].rearrange("p g q f -> p (g q) f")
                sp.dma_start(x_blocks[:, 0:NB - 1, :], x[0:main, :].rearrange("(b p) f -> p b f", p=P)).then_inc(x_again, 16)
                sp.wait_ge(x_clear, 1)
                sp.dma_start(x_blocks[0:NTAIL, NB - 1, :], x[main:N, :]).then_inc(x_again, 16)
                with sp.Fori(1, STEPS // BODY) as g:
                    for q in range(BODY // 2):
                        load(g, q, True)

            POOLS = 2

            def before_one_hot(eng, g, k):
                if k % 2 == 0:
                    eng.wait_ge(rows_in[k // 2], 16 * (g + 1))
                if from_(g, k, BODY):
                    eng.wait_ge(sum_mm, BODY * g + k - BODY + 1)

            def numbers(k):
                return rec2[:, k, :, :, M:RW].rearrange("p u j o -> p (u j) o")

            @block.gpsimd
            def _(pool):
                pool.memset(xf[:, NG - 1, LB - 1, :], 0.0).then_inc(x_clear, 1)
                pool.memset(acc[:, :, :], 0.0).then_inc(acc_clear, 1)

                def step(g, k):
                    ahead = shift(g, k, 2)
                    if inside(*ahead):
                        before_one_hot(pool, *ahead)
                        pool.sem_inc(hot_turns, 1)
                        for j in range(J2 - POOLS, J2):
                            last = pool.tensor_scalar(lhot[:, ahead[1], j, :], iota[:, :], numbers(ahead[1])[:, j, :], None, ALU.is_equal)
                        last.then_inc(lo_hot[1], 1)
                    if inside(*shift(g, k, -2)):
                        q = (k - 2) % BODY
                        pool.wait_ge(msg_m, BODY * g + k - 1)
                        pool.tensor_tensor(out=msgp[:, q, 2, :, :], in0=msgr[:, q % 2, :, :], in1=msgp[:, q, 1, :, :],
                                           op=ALU.subtract).then_inc(msg_l, 1)
                in_bodies(pool, step)

            @block.tensor
            def _(pe):
                te = nc.tensor
                bucket = [pe.alloc_register(f"pe_bucket{u}") for u in range(HOLD * U)]
                held = []

                def turn(g, k):
                    if not inside(g, k):
                        return
                    s = BODY * g + k
                    for made in lo_hot:
                        pe.wait_ge(made, s + 1)
                    if from_(g, k, 2):
                        pe.wait_ge(lo_hot_out, s - 1)
                    for j in range(J2):
                        last = te.transpose(psumb[:, k % 2, j * P:(j + 1) * P], lhot[:, k, j, :], ident[:, :])
                    last.then_inc(lo_hot_t, 1)

                def add_a(g, k, bs):
                    s = BODY * g + k
                    pe.wait_ge(lo_hot_out, s + 1)
                    if from_(g, k, 2):
                        pe.wait_ge(msg_sum, s - 1)
                    for j in range(J2):
                        for part in range(3):
                            last = te.matmul(psum[:, 2 + k % 2, j * M:(j + 1) * M], lhot_t[:, k % 2, j, :],
                                             a_tab[:, ds(bs[j // J], 1), part, :].rearrange("p o m -> p (o m)"),
                                             start=j == 0 and part == 0, stop=j == J2 - 1 and part == 2)
                    last.then_inc(a_mm, 1)

                def sum_up(g, k):
                    if not inside(g, k):
                        return
                    s = BODY * g + k
                    pe.wait_ge(msg_l, s + 1)
                    if from_(g, k, 2):
                        pe.wait_ge(acc_second, s - 1)
                    for j in range(J2):
                        u = j // J
                        for part in range(3):
                            last = te.matmul(psum[:, 4 + k % 2, u * M:(u + 1) * M], lhot[:, k, j, :], msgp[:, k, part, j, :],
                                             start=j == 0 and part == 0, stop=j == J2 - 1 and part == 2)
                    last.then_inc(sum_mm, 1)

                def step(g, k):
                    if inside(g, k) and k % HOLD == 0:
                        pe.load(bucket, bucket_row[0:1, ds((BODY * g + k) * U, HOLD * U)])
                        held[:] = [pe.snap(b, min_val=0, max_val=SPARE) for b in bucket]
                    turn(*shift(g, k, 1))
                    if inside(g, k):
                        add_a(g, k, held[k % HOLD * U:][:U])
                    sum_up(*shift(g, k, -3))
                in_bodies(pe, step)

            @block.scalar
            def _(act):
                def step(g, k):
                    if inside(*shift(g, k, 1)):
                        s, q = BODY * g + k + 1, (k + 1) % 2
                        act.wait_ge(lo_hot_t, s + 1)
                        if from_(*shift(g, k, 1), 2):
                            act.wait_ge(a_mm, s - 1)
                        nc.scalar.copy(lhot_t[:, q, :, :].rearrange("p j e -> p (j e)"), psumb[:, q, 0:J2 * P]).then_inc(lo_hot_out, 1)
                    if inside(*shift(g, k, -1)):
                        q = (k - 1) % BODY
                        act.wait_ge(msg_r, BODY * g + k)
                        nc.scalar.copy(msgp[:, q, 1, :, :], msgr[:, q % 2, :, :]).then_inc(msg_m, 1)
                    if inside(g, k):
                        s = BODY * g + k
                        act.wait_ge(msg_sum, s + 1)
                        if from_(g, k, BODY):
                            act.wait_ge(sum_mm, s - BODY + 1)
                        nc.scalar.activation(msgp[:, k, 0, :, :], msg[:, k % 2, :, :], ACT.Relu).then_inc(msg_h, 1)
                in_bodies(act, step)

            @block.vector
            def _(dve):
                v = nc.vector
                bucket = [dve.alloc_register(f"dve_bucket{u}") for u in range(HOLD * U)]
                held = []
                dve.wait_ge(acc_clear, 1)

                def add_sum(k, bs, u, signal):
                    a = acc[:, ds(bs[u], 1), :].rearrange("p o m -> p (o m)")
                    v.tensor_tensor(out=a, in0=a, in1=psum[:, 4 + k % 2, u * M:(u + 1) * M], op=ALU.add).then_inc(signal, 1)

                def flat(t):
                    return t.rearrange("p j m -> p (j m)")

                def step(g, k):
                    s = BODY * g + k
                    done = inside(*shift(g, k, -4))
                    ahead = shift(g, k, 2)
                    if inside(*ahead):
                        before_one_hot(dve, *ahead)
                        n = J2 - POOLS
                        v.tensor_tensor(out=lhot[:, ahead[1], 0:n, :], in0=iota[:, :].unsqueeze(1).broadcast_to([P, n, P]),
                                        in1=numbers(ahead[1])[:, 0:n, :].broadcast_to([P, n, P]), op=ALU.is_equal).then_inc(lo_hot[0], 1)
                    if done and k % HOLD == 0:
                        dve.load(bucket, bucket_row[0:1, ds((s - 4) * U, HOLD * U)])
                        held[:] = [dve.snap(b, min_val=0, max_val=SPARE) for b in bucket]
                    bs = held[k % HOLD * U:][:U]
                    if done:
                        dve.wait_ge(sum_mm, s - 3)
                        if from_(g, k, 5):
                            dve.wait_ge(acc_second, s - 4)
                        add_sum(k, bs, 0, acc_first)
                    if inside(*shift(g, k, -1)):
                        q = (k - 1) % BODY
                        dve.wait_ge(msg_h, s)
                        if from_(g, k, 3):
                            dve.wait_ge(msg_l, s - 2)
                        v.scalar_tensor_tensor(out=flat(msgr[:, q % 2, :, :]), in0=flat(msg[:, q % 2, :, :]), scalar=0.0,
                                               in1=flat(msgp[:, q, 0, :, :]), op0=ALU.max, op1=ALU.subtract).then_inc(msg_r, 1)
                    if done:
                        dve.wait_ge(acc_first, s - 3)
                        add_sum(k, bs, 1, acc_second)
                    if inside(g, k):
                        dve.wait_ge(a_mm, s + 1)
                        if from_(g, k, 2):
                            dve.wait_ge(msg_r, s - 1)
                        v.tensor_tensor(out=msg[:, k % 2, :, :], in0=psum[:, 2 + k % 2, 0:J2 * M].rearrange("p (j m) -> p j m", j=J2),
                                        in1=rec2[:, k, :, :, 0:M].rearrange("p u j m -> p (u j) m"), op=ALU.add).then_inc(msg_sum, 1)
                in_bodies(dve, step)

        sums_t, sums_out, y_mm = sem("sums_t"), sem("sums_out"), sem("y_mm")
        z_ready, y_ready, y_out, x_free = sem("z_ready"), sem("y_ready"), sem("y_out"), sem("x_free")
        with ExitStack() as tmp:
            st = sb("st", [P, 2, P], f32, tmp)
            z = sb("z", [P, 2, FG * F], f32, tmp)
            cp = sb("cp", [P, 2, P], f32, tmp)
            sums_cp = sem("sums_cp")
            assert NG % 2 == 1

            def finish(eng, step):
                for k in range(2):
                    step(k, k, FG)
                with eng.Fori(1, NG // 2) as i:
                    for k in range(2):
                        step(2 * i + k, k, FG)
                step(NG - 1, 0, LB)

            block = tmp.enter_context(nc.Block())

            @block.sync
            def _(sp):
                main = (NB - 1) * P
                with sp.Fori(0, NG - 1) as g:
                    sp.wait_ge(y_ready, g + 1)
                    sp.dma_start(y[ds(g * (FG * P), FG * P), :].rearrange("(q p) f -> p q f", p=P),
                                 xf[:, ds(g, 1), :, :].rearrange("p o q f -> p (o q) f")).then_inc(y_out, 16)
                sp.wait_ge(y_ready, NG)
                r0 = (NG - 1) * FG * P
                sp.dma_start(y[r0:main, :].rearrange("(q p) f -> p q f", p=P), xf[:, NG - 1, 0:LB - 1, :]).then_inc(y_out, 16)
                sp.dma_start(y[main:N, :], xf[0:NTAIL, NG - 1, LB - 1, :]).then_inc(y_out, 16)
                sp.wait_ge(y_out, 16 * (NG + 1))

            @block.tensor
            def _(pe):
                def step(g, k, nb):
                    later = not (isinstance(g, int) and g < 2)
                    pe.wait_ge(sums_cp, g + 1)
                    if later:
                        pe.wait_ge(sums_out, g - 1)
                    nc.tensor.transpose(psum[:, k, 0:P], cp[:, k, :], identf[:, :]).then_inc(sums_t, 1)
                    pe.wait_ge(sums_out, g + 1)
                    if later:
                        pe.wait_ge(z_ready, g - 1)
                    nc.tensor.matmul(psum[:, 2 + k, 0:nb * F], st[:, k, :],
                                     w_sum[:, 0:nb, :].rearrange("p q f -> p (q f)"), start=True, stop=True).then_inc(y_mm, 1)
                finish(pe, step)

            @block.scalar
            def _(act):
                def copy(g, k):
                    later = not (isinstance(g, int) and g < 2)
                    if later:
                        act.wait_ge(sums_t, g - 1)
                    nc.scalar.copy(cp[:, k, :], acc[:, ds(g * FG, FG), :].rearrange("p q m -> p (q m)")).then_inc(sums_cp, 1)

                def step(g, k, nb):
                    later = not (isinstance(g, int) and g < 2)
                    copy(g, k)
                    act.wait_ge(sums_t, g + 1)
                    if later:
                        act.wait_ge(y_mm, g - 1)
                    nc.scalar.copy(st[:, k, :], psum[:, k, 0:P]).then_inc(sums_out, 1)
                finish(act, step)

            @block.vector
            def _(dve):
                v = nc.vector
                dve.wait_ge(x_again, 32)

                def step(g, k, nb):
                    later = not (isinstance(g, int) and g < 2)
                    dve.wait_ge(y_mm, g + 1)
                    if later:
                        dve.wait_ge(y_ready, g - 1)
                    v.tensor_tensor(out=z[:, k, 0:nb * F], in0=psum[:, 2 + k, 0:nb * F],
                                    in1=ypart[:, ds(g * FG, nb), :].rearrange("p q f -> p (q f)"), op=ALU.add).then_inc(z_ready, 1)
                    dve.wait_ge(z_ready, g + 1)
                    xg = xf[:, ds(g, 1), 0:nb, :].rearrange("p o q f -> p (o q f)")
                    v.scalar_tensor_tensor(out=xg, in0=z[:, k, 0:nb * F], scalar=0.0, in1=xg, op0=ALU.max, op1=ALU.add)\
                        .then_inc(y_ready, 1)
                finish(dve, step)


def kernel(x, src, dst, edge_attr_64, L0_gnn_W_edge, L0_gnn_b_edge, L0_gnn_W_node, L0_gnn_b_node):
    import numpy as np
    import concourse.bacc as bacc
    from concourse import mybir as mb
    from concourse.bass_utils import run_bass_kernel_spmd

    ins = {"x": x, "src": src, "dst": dst, "edge_attr": edge_attr_64, "w_edge": L0_gnn_W_edge,
           "b_edge": L0_gnn_b_edge, "w_node": L0_gnn_W_node, "b_node": L0_gnn_b_node}
    nc = bacc.Bacc("TRN2", target_bir_lowering=False, num_devices=1)
    arrays, aps = {}, []
    for name, a in ins.items():
        a = np.ascontiguousarray(a)
        arrays[name] = a
        aps.append(nc.dram_tensor(name, a.shape, mb.dt.from_np(a.dtype), kind="ExternalInput").ap())
    out = nc.dram_tensor("y", tuple(x.shape), mb.dt.float32, kind="ExternalOutput").ap()
    gnn_layer(nc, *aps, out)
    r = run_bass_kernel_spmd(nc, [arrays], core_ids=[0])
    return r.results[0]["y"]
```
